# Optimizing a Trainium2 kernel written in Bass

```python
import numpy as np
import jax
import jax.numpy as jnp

def _softmax(x, axis=-1):
    return jax.nn.softmax(x, axis=axis)

def _gelu(x):
    return jax.nn.gelu(x, approximate=True)

def _silu(x):
    return jax.nn.silu(x)

def _sigmoid(x):
    return jax.nn.sigmoid(x)

def _layernorm(x, axis=-1, eps=1e-05):
    m = jnp.mean(x, axis=axis, keepdims=True)
    v = jnp.var(x, axis=axis, keepdims=True)
    return (x - m) / jnp.sqrt(v + eps)

def _scatter_add(tgt, idx, src, axis=0):
    return tgt.at[idx].add(src)

def _segment_sum(src, seg, n):
    return jax.ops.segment_sum(src, seg, n)
kernel_name = 'mk_dlrm_tower_d1_rec_r8_4cd01a'

def setup_inputs(seed: int=0):
    np.random.seed(seed)
    _w = jnp.asarray

    def _rec_inputs():
        import jax
        import jax.numpy as jnp
        _tk = jax.random.key(seed)
        dense_ctx = jax.random.normal(jax.random.fold_in(_tk, 190), (512, 16), jnp.float32)
        ids = jnp.stack([jax.random.randint(jax.random.fold_in(_tk, 200 + f), (512,), 0, v, jnp.int32) for f, v in enumerate([1000, 12500, 1250, 125000, 1250, 1250, 125000, 1000, 1250, 1250, 12500, 1000, 1250, 12500, 12500, 125000, 12500, 12500, 12500, 125000, 12500, 12500, 1000, 1000, 12500, 1000, 1250, 1000, 1000, 1250, 12500, 125000, 1000, 12500, 125000, 12500, 1000, 12500, 12500, 1000])], axis=1)
        tbl_0 = 0.05 * jax.random.normal(jax.random.fold_in(_tk, 500 + 0), (1000, 32), jnp.float32)
        tbl_1 = 0.05 * jax.random.normal(jax.random.fold_in(_tk, 500 + 1), (12500, 32), jnp.float32)
        tbl_2 = 0.05 * jax.random.normal(jax.random.fold_in(_tk, 500 + 2), (1250, 32), jnp.float32)
        tbl_3 = 0.05 * jax.random.normal(jax.random.fold_in(_tk, 500 + 3), (125000, 32), jnp.float32)
        tbl_4 = 0.05 * jax.random.normal(jax.random.fold_in(_tk, 500 + 4), (1250, 32), jnp.float32)
        tbl_5 = 0.05 * jax.random.normal(jax.random.fold_in(_tk, 500 + 5), (1250, 32), jnp.float32)
        tbl_6 = 0.05 * jax.random.normal(jax.random.fold_in(_tk, 500 + 6), (125000, 32), jnp.float32)
        tbl_7 = 0.05 * jax.random.normal(jax.random.fold_in(_tk, 500 + 7), (1000, 32), jnp.float32)
        tbl_8 = 0.05 * jax.random.normal(jax.random.fold_in(_tk, 500 + 8), (1250, 32), jnp.float32)
        tbl_9 = 0.05 * jax.random.normal(jax.random.fold_in(_tk, 500 + 9), (1250, 32), jnp.float32)
        tbl_10 = 0.05 * jax.random.normal(jax.random.fold_in(_tk, 500 + 10), (12500, 32), jnp.float32)
        tbl_11 = 0.05 * jax.random.normal(jax.random.fold_in(_tk, 500 + 11), (1000, 32), jnp.float32)
        tbl_12 = 0.05 * jax.random.normal(jax.random.fold_in(_tk, 500 + 12), (1250, 32), jnp.float32)
        tbl_13 = 0.05 * jax.random.normal(jax.random.fold_in(_tk, 500 + 13), (12500, 32), jnp.float32)
        tbl_14 = 0.05 * jax.random.normal(jax.random.fold_in(_tk, 500 + 14), (12500, 32), jnp.float32)
        tbl_15 = 0.05 * jax.random.normal(jax.random.fold_in(_tk, 500 + 15), (125000, 32), jnp.float32)
        tbl_16 = 0.05 * jax.random.normal(jax.random.fold_in(_tk, 500 + 16), (12500, 32), jnp.float32)
        tbl_17 = 0.05 * jax.random.normal(jax.random.fold_in(_tk, 500 + 17), (12500, 32), jnp.float32)
        tbl_18 = 0.05 * jax.random.normal(jax.random.fold_in(_tk, 500 + 18), (12500, 32), jnp.float32)
        tbl_19 = 0.05 * jax.random.normal(jax.random.fold_in(_tk, 500 + 19), (125000, 32), jnp.float32)
        tbl_20 = 0.05 * jax.random.normal(jax.random.fold_in(_tk, 500 + 20), (12500, 32), jnp.float32)
        tbl_21 = 0.05 * jax.random.normal(jax.random.fold_in(_tk, 500 + 21), (12500, 32), jnp.float32)
        tbl_22 = 0.05 * jax.random.normal(jax.random.fold_in(_tk, 500 + 22), (1000, 32), jnp.float32)
        tbl_23 = 0.05 * jax.random.normal(jax.random.fold_in(_tk, 500 + 23), (1000, 32), jnp.float32)
        tbl_24 = 0.05 * jax.random.normal(jax.random.fold_in(_tk, 500 + 24), (12500, 32), jnp.float32)
        tbl_25 = 0.05 * jax.random.normal(jax.random.fold_in(_tk, 500 + 25), (1000, 32), jnp.float32)
        tbl_26 = 0.05 * jax.random.normal(jax.random.fold_in(_tk, 500 + 26), (1250, 32), jnp.float32)
        tbl_27 = 0.05 * jax.random.normal(jax.random.fold_in(_tk, 500 + 27), (1000, 32), jnp.float32)
        tbl_28 = 0.05 * jax.random.normal(jax.random.fold_in(_tk, 500 + 28), (1000, 32), jnp.float32)
        tbl_29 = 0.05 * jax.random.normal(jax.random.fold_in(_tk, 500 + 29), (1250, 32), jnp.float32)
        tbl_30 = 0.05 * jax.random.normal(jax.random.fold_in(_tk, 500 + 30), (12500, 32), jnp.float32)
        tbl_31 = 0.05 * jax.random.normal(jax.random.fold_in(_tk, 500 + 31), (125000, 32), jnp.float32)
        tbl_32 = 0.05 * jax.random.normal(jax.random.fold_in(_tk, 500 + 32), (1000, 32), jnp.float32)
        tbl_33 = 0.05 * jax.random.normal(jax.random.fold_in(_tk, 500 + 33), (12500, 32), jnp.float32)
        tbl_34 = 0.05 * jax.random.normal(jax.random.fold_in(_tk, 500 + 34), (125000, 32), jnp.float32)
        tbl_35 = 0.05 * jax.random.normal(jax.random.fold_in(_tk, 500 + 35), (12500, 32), jnp.float32)
        tbl_36 = 0.05 * jax.random.normal(jax.random.fold_in(_tk, 500 + 36), (1000, 32), jnp.float32)
        tbl_37 = 0.05 * jax.random.normal(jax.random.fold_in(_tk, 500 + 37), (12500, 32), jnp.float32)
        tbl_38 = 0.05 * jax.random.normal(jax.random.fold_in(_tk, 500 + 38), (12500, 32), jnp.float32)
        tbl_39 = 0.05 * jax.random.normal(jax.random.fold_in(_tk, 500 + 39), (1000, 32), jnp.float32)
        _rk = jax.random.fold_in(_tk, 7)
        W_top1 = 0.0354441 * jax.random.normal(jax.random.fold_in(_tk, 801), (796, 512), jnp.float32)
        W_top2 = 0.0441942 * jax.random.normal(jax.random.fold_in(_tk, 802), (512, 256), jnp.float32)
        W_top3 = 0.0625 * jax.random.normal(jax.random.fold_in(_tk, 803), (256, 1), jnp.float32)
        b_top1 = jnp.zeros((512,), jnp.float32)
        b_top2 = jnp.zeros((256,), jnp.float32)
        return (dense_ctx, ids, tbl_0, tbl_1, tbl_2, tbl_3, tbl_4, tbl_5, tbl_6, tbl_7, tbl_8, tbl_9, tbl_10, tbl_11, tbl_12, tbl_13, tbl_14, tbl_15, tbl_16, tbl_17, tbl_18, tbl_19, tbl_20, tbl_21, tbl_22, tbl_23, tbl_24, tbl_25, tbl_26, tbl_27, tbl_28, tbl_29, tbl_30, tbl_31, tbl_32, tbl_33, tbl_34, tbl_35, tbl_36, tbl_37, tbl_38, tbl_39, W_top1, b_top1, W_top2, b_top2, W_top3)
    dense_ctx, ids, tbl_0, tbl_1, tbl_2, tbl_3, tbl_4, tbl_5, tbl_6, tbl_7, tbl_8, tbl_9, tbl_10, tbl_11, tbl_12, tbl_13, tbl_14, tbl_15, tbl_16, tbl_17, tbl_18, tbl_19, tbl_20, tbl_21, tbl_22, tbl_23, tbl_24, tbl_25, tbl_26, tbl_27, tbl_28, tbl_29, tbl_30, tbl_31, tbl_32, tbl_33, tbl_34, tbl_35, tbl_36, tbl_37, tbl_38, tbl_39, W_top1, b_top1, W_top2, b_top2, W_top3 = _rec_inputs()

    def _L0_rec_setup():
        import jax, jax.numpy as jnp
        import numpy as np
        NUM_FIELDS = 40
        _I_IDX, _J_IDX = np.triu_indices(NUM_FIELDS, k=1)
        key = jax.random.key(seed)
        k1, k2 = jax.random.split(key)
        batch, num_fields, embed_dim = (1024, NUM_FIELDS, 32)
        num_interactions = num_fields * (num_fields - 1) // 2
        embeddings = jax.random.normal(k1, (batch, num_fields, embed_dim), dtype=jnp.float32)
        W = jax.random.normal(k2, (num_interactions, embed_dim, embed_dim), dtype=jnp.float32)
        return {'embeddings': embeddings, 'W': W}
    _L0_rec_all = _L0_rec_setup()
    _L0_rec_in = {k: v for k, v in _L0_rec_all.items() if k in ('W',)}
    del _L0_rec_all
    return {'dense_ctx': dense_ctx, 'ids': ids, 'tbl_0': tbl_0, 'tbl_1': tbl_1, 'tbl_2': tbl_2, 'tbl_3': tbl_3, 'tbl_4': tbl_4, 'tbl_5': tbl_5, 'tbl_6': tbl_6, 'tbl_7': tbl_7, 'tbl_8': tbl_8, 'tbl_9': tbl_9, 'tbl_10': tbl_10, 'tbl_11': tbl_11, 'tbl_12': tbl_12, 'tbl_13': tbl_13, 'tbl_14': tbl_14, 'tbl_15': tbl_15, 'tbl_16': tbl_16, 'tbl_17': tbl_17, 'tbl_18': tbl_18, 'tbl_19': tbl_19, 'tbl_20': tbl_20, 'tbl_21': tbl_21, 'tbl_22': tbl_22, 'tbl_23': tbl_23, 'tbl_24': tbl_24, 'tbl_25': tbl_25, 'tbl_26': tbl_26, 'tbl_27': tbl_27, 'tbl_28': tbl_28, 'tbl_29': tbl_29, 'tbl_30': tbl_30, 'tbl_31': tbl_31, 'tbl_32': tbl_32, 'tbl_33': tbl_33, 'tbl_34': tbl_34, 'tbl_35': tbl_35, 'tbl_36': tbl_36, 'tbl_37': tbl_37, 'tbl_38': tbl_38, 'tbl_39': tbl_39, 'W_top1': W_top1, 'b_top1': b_top1, 'W_top2': W_top2, 'b_top2': b_top2, 'W_top3': W_top3, 'L0_rec_W': _L0_rec_in['W']}

def reference(dense_ctx, ids, tbl_0, tbl_1, tbl_2, tbl_3, tbl_4, tbl_5, tbl_6, tbl_7, tbl_8, tbl_9, tbl_10, tbl_11, tbl_12, tbl_13, tbl_14, tbl_15, tbl_16, tbl_17, tbl_18, tbl_19, tbl_20, tbl_21, tbl_22, tbl_23, tbl_24, tbl_25, tbl_26, tbl_27, tbl_28, tbl_29, tbl_30, tbl_31, tbl_32, tbl_33, tbl_34, tbl_35, tbl_36, tbl_37, tbl_38, tbl_39, W_top1, b_top1, W_top2, b_top2, W_top3, L0_rec_W):
    import jax
    import jax.numpy as jnp

    def _L0_rec_ref(embeddings, W):
        import jax, jax.numpy as jnp
        import numpy as np
        NUM_FIELDS = 40
        _I_IDX, _J_IDX = np.triu_indices(NUM_FIELDS, k=1)
        vi = embeddings[:, _I_IDX, :]
        vj = embeddings[:, _J_IDX, :]
        return jnp.einsum('bke,kef,bkf->bk', vi, W, vj)
    e = jnp.stack([tbl_0[ids[:, 0]], tbl_1[ids[:, 1]], tbl_2[ids[:, 2]], tbl_3[ids[:, 3]], tbl_4[ids[:, 4]], tbl_5[ids[:, 5]], tbl_6[ids[:, 6]], tbl_7[ids[:, 7]], tbl_8[ids[:, 8]], tbl_9[ids[:, 9]], tbl_10[ids[:, 10]], tbl_11[ids[:, 11]], tbl_12[ids[:, 12]], tbl_13[ids[:, 13]], tbl_14[ids[:, 14]], tbl_15[ids[:, 15]], tbl_16[ids[:, 16]], tbl_17[ids[:, 17]], tbl_18[ids[:, 18]], tbl_19[ids[:, 19]], tbl_20[ids[:, 20]], tbl_21[ids[:, 21]], tbl_22[ids[:, 22]], tbl_23[ids[:, 23]], tbl_24[ids[:, 24]], tbl_25[ids[:, 25]], tbl_26[ids[:, 26]], tbl_27[ids[:, 27]], tbl_28[ids[:, 28]], tbl_29[ids[:, 29]], tbl_30[ids[:, 30]], tbl_31[ids[:, 31]], tbl_32[ids[:, 32]], tbl_33[ids[:, 33]], tbl_34[ids[:, 34]], tbl_35[ids[:, 35]], tbl_36[ids[:, 36]], tbl_37[ids[:, 37]], tbl_38[ids[:, 38]], tbl_39[ids[:, 39]]], axis=1)
    z = _L0_rec_ref(e, L0_rec_W)
    z = z.reshape(z.shape[0], -1)
    h = jnp.concatenate([z, dense_ctx], axis=1)
    h = jnp.maximum(h @ W_top1 + b_top1, 0.0)
    h = jnp.maximum(h @ W_top2 + b_top2, 0.0)
    y = h @ W_top3
    return y

_drawn_inputs = setup_inputs


def setup_inputs(seed=0):
    import zlib

    import numpy as np

    out = dict(_drawn_inputs(seed))
    spreads = {'b_top1': (0.0, 0.1), 'b_top2': (0.0, 0.1)}
    factors = {}
    for name, (base, spread) in spreads.items():
        noise = np.random.default_rng([zlib.crc32(name.encode()), seed]).standard_normal(out[name].shape)
        drawn = base * np.exp(spread * noise) if base else spread * noise
        out[name] = jnp.asarray(drawn.astype(out[name].dtype))
    for name, factor in factors.items():
        out[name] = (out[name] * factor).astype(out[name].dtype)
    return out
```

```python
from contextlib import ExitStack

import numpy as np

import concourse.bass as bass
from concourse import mybir

F32 = mybir.dt.float32
F32R = mybir.dt.float32r
I32 = mybir.dt.int32
U32 = mybir.dt.uint32
ALU = mybir.AluOpType
ACT = mybir.ActivationFunctionType
AX_X = mybir.AxisListType.X

P = 128
BATCH, FIELDS, EMB, DENSE = 512, 40, 32, 16
HID1, HID2 = 512, 256
HALVES = 2
HB = BATCH // HALVES
BT = HB // P
PER = P // EMB
GROUPS = FIELDS // PER

ROW_GROUPS = [0, 0, 1, 1, 2, 2, 3, 4, 5, 6]
CHUNKS = PER * sum(ROW_GROUPS)
ROW_TILES = CHUNKS * PER // P
assert ROW_TILES * P == CHUNKS * PER
MAX_CHUNKS = 4
Y_GROUPS = max(ROW_GROUPS)

PAIRS = FIELDS * (FIELDS - 1) // 2
COL_PAIRS = PAIRS - CHUNKS * PER
COL_K = COL_PAIRS + DENSE
COL_TILES = -(-COL_K // P)
K_TILES = ROW_TILES + COL_TILES
K_ROWS = ROW_TILES * P + COL_K
MAX_COL_PAIRS = max(i - PER * ROW_GROUPS[i // PER] for i in range(FIELDS))

W_COLS = PAIRS * EMB
PIECES = 12
PIECE = W_COLS // PIECES
QUARTER = PIECE // PER
assert QUARTER * PER * PIECES == W_COLS

T_SLOTS, ROW_SLOTS, COL_SLOTS, STACK_SLOTS = 2, 2, 2, 4
BANK = 512
LEAD = STACK_SLOTS - 1
STEPS = HALVES * FIELDS


def w_at(i):
    return EMB * i * (i - 1) // 2


def units_of(i):
    rows = ROW_GROUPS[i // PER]
    units = [("cols", PER * rows, i)] if i > PER * rows else []
    parts = -(-rows // MAX_CHUNKS)
    ends = [-(-rows * (k + 1) // parts) for k in range(parts)]
    return units + [("rows", a, b) for a, b in zip([0] + ends, ends)]


UNITS = [u for i in range(FIELDS) for u in units_of(i)]
FIRST_UNIT = [len([u for k in range(i) for u in units_of(k)]) for i in range(FIELDS + 1)]
N_UNITS = len(UNITS)


def pair_order():
    rows, cols = [None] * (CHUNKS * PER), []
    n = 0
    for kind, a, b, i in [(*u, i) for i in range(FIELDS) for u in units_of(i)]:
        if kind == "cols":
            cols += [(j, i) for j in range(a, b)]
            continue
        for g in range(a, b):
            for r in range(PER):
                rows[z_row(n) + r] = (PER * g + r, i)
            n += 1
    return rows + cols


def z_row(n):
    return n // 32 * P + n % 4 * 32 + n % 32 // 4 * PER


MLP_T = list(range(COL_TILES))
MLP_H1 = [MLP_T[-1] + 1 + n for n in range(HID1 // P)]
MLP_H2 = [MLP_H1[-1] + 1 + n for n in range(HID2 // P)]
MLP_Y = MLP_H2[-1] + 1
MLP_STEPS = MLP_Y + 1
MLP_FROM = FIELDS + 4


def side_jobs_at(n):
    jobs = []
    for m in (range(LEAD + 1) if n == 0 else [n + LEAD]):
        if m < STEPS:
            g = m % FIELDS // PER
            jobs.append(("stack", m))
            if m % PER == 0 and g < Y_GROUPS:
                jobs.append(("turn", m // PER))
    if MLP_FROM <= n < MLP_FROM + MLP_STEPS:
        jobs.append(("mlp", 0, n - MLP_FROM))
    if n == STEPS:
        jobs += [("mlp", 1, s) for s in range(MLP_STEPS)]
    return jobs


SIDE_JOBS = [job for n in range(STEPS + 1) for job in side_jobs_at(n)]
SIDE = {job: k for k, job in enumerate(SIDE_JOBS)}


def split_at(n):
    first = range(0, LEAD + 2) if n == 0 else [n + LEAD + 1]
    return [m // PER for m in first if m < STEPS and m % PER == 0]


def pieces_at(n):
    def when(s):
        first_reader = min(i for i in range(FIELDS) if w_at(i + 1) > s * PIECE)
        return max(0, first_reader - 9)
    return [s for s in range(PIECES) if when(s) == n]


def program(nc, ids, tables, dense, w_pieces, w1, b1, w2, b2, w3, eye, strips, out):
    with ExitStack() as ctx:
        def sb(name, shape, dt=F32):
            return ctx.enter_context(nc.sbuf_tensor(name, shape, dt))

        def psum(name, shape):
            return ctx.enter_context(nc.psum_tensor(name, shape, F32))

        def sem(name):
            return ctx.enter_context(nc.semaphore(name))

        ids_sb = sb("ids_sb", [P, HALVES * BT, FIELDS], I32)
        x = sb("x", [P, HALVES, BT, FIELDS * EMB])
        x_parts = sb("x_parts", [P, 2, BT, PER, 4, EMB], F32R)
        x_stack = sb("x_stack", [P, STACK_SLOTS, HB], F32R)
        x_turned = sb("x_turned", [P, HALVES, Y_GROUPS, HB])
        w_raw = sb("w_raw", [P, 2, QUARTER])
        w_hi = sb("w_hi", [P, 2, QUARTER], F32R)
        w_stack = sb("w_stack", [P, W_COLS], F32R)
        row_prod = sb("row_prod", [P, ROW_SLOTS, MAX_CHUNKS, HB])
        col_prod = sb("col_prod", [P, COL_SLOTS, BT, MAX_COL_PAIRS * EMB])
        z_cols = sb("z_cols", [P, HALVES, BT, COL_K])
        z_t = sb("z_t", [P, K_TILES, HB])
        w1_sb = sb("w1_sb", [P, K_TILES, HID1])
        w2_sb = sb("w2_sb", [P, HID1 // P, HID2])
        w3_sb = sb("w3_sb", [P, HID2 // P])
        b1_sb = sb("b1_sb", [P, HID1 // P])
        b2_sb = sb("b2_sb", [P, HID2 // P])
        h1 = sb("h1", [P, HID1 // P, HB])
        h2 = sb("h2", [P, HID2 // P, HB])
        y_sb = sb("y_sb", [1, HALVES, HB])
        eye_sb = sb("eye_sb", [P, P])
        eye_r = sb("eye_r", [P, P], F32R)
        strips_sb = sb("strips_sb", [P, 2 * EMB - PER])

        t_ps = psum("t_ps", [P, T_SLOTS, 2, BANK])
        side_ps = psum("side_ps", [P, 2, BANK])
        z_ps = psum("z_ps", [P, 2, BANK])

        ids_loaded = sem("ids_loaded")
        dense_loaded = sem("dense_loaded")
        consts_loaded = sem("consts_loaded")
        mlp_loaded = sem("mlp_loaded")
        gathered = [sem(f"gathered_{g}") for g in range(GROUPS)]
        w_loaded = [sem(f"w_loaded_{s}") for s in range(2)]
        w_hi_ready = sem("w_hi_ready")
        w_lo_ready = sem("w_lo_ready")
        w_stacked = [sem(f"w_stacked_{s}") for s in range(2)]
        eye_ready = sem("eye_ready")
        x_hi_ready = sem("x_hi_ready")
        x_lo_ready = sem("x_lo_ready")
        x_parts_ready = sem("x_parts_ready")
        side_filled = sem("side_filled")
        side_drained = sem("side_drained")
        t_filled = sem("t_filled")
        multiplied = sem("multiplied")
        cols_summed = sem("cols_summed")
        rows_summed = sem("rows_summed")
        z_drained = sem("z_drained")
        stored = sem("stored")

        def wait_count(eng, s, value):
            if value > 0:
                eng.wait_ge(s, value)

        row_units = [n for n in range(HALVES * N_UNITS) if UNITS[n % N_UNITS][0] == "rows"]
        row_index = {n: k for k, n in enumerate(row_units)}
        col_units = [n for n in range(HALVES * N_UNITS) if UNITS[n % N_UNITS][0] == "cols"]
        col_index = {n: k for k, n in enumerate(col_units)}
        first_chunk, chunk = {}, 0
        for n in row_units:
            first_chunk[n] = chunk
            chunk += UNITS[n % N_UNITS][2] - UNITS[n % N_UNITS][1]
        last_row_unit = {}
        for n in row_units:
            _, a, b = UNITS[n % N_UNITS]
            for m in range(first_chunk[n], first_chunk[n] + b - a):
                last_row_unit[m // 32] = n
        col_at, at = {}, 0
        for n in col_units[:len(col_units) // HALVES]:
            col_at[n] = at
            at += UNITS[n][2] - UNITS[n][1]

        def units_at(n):
            half, i = divmod(n, FIELDS)
            return range(half * N_UNITS + FIRST_UNIT[i], half * N_UNITS + FIRST_UNIT[i + 1])

        def units_until(n):
            return n // FIELDS * N_UNITS + FIRST_UNIT[n % FIELDS + 1] if n >= 0 else 0

        def wait_w_columns(eng, end):
            s = (end - 1) // PIECE
            eng.wait_ge(w_stacked[s % 2], 16 * PER * PER * (s // 2 + 1))
            if s > 0:
                eng.wait_ge(w_stacked[(s - 1) % 2], 16 * PER * PER * ((s - 1) // 2 + 1))

        def last_job_of_group(gg):
            return SIDE["stack", PER * gg + PER - 1]

        def sums_after(u):
            return [v for v in row_units if v == u - 2]

        sum_step = {v: n for n in range(STEPS) for u in units_at(n) for v in sums_after(u)}

        def z_tiles_at(n):
            return [t for t, u in last_row_unit.items() if min(STEPS, sum_step.get(u, STEPS) + 1) == n]

        block = ctx.enter_context(nc.Block())

        @block.sync
        def _(sp):
            sp.dma_start(ids_sb[:], ids.rearrange("(t p) f -> p t f", p=P)).then_inc(ids_loaded, 16)

            def load_piece(s):
                if s >= 2:
                    sp.wait_ge(w_stacked[s % 2], 16 * PER * PER * (s // 2))
                sp.dma_start(w_raw[:, s % 2, :], w_pieces[s]).then_inc(w_loaded[s % 2], 16)

            load_piece(0)
            load_piece(1)
            sp.dma_start(eye_sb[:], eye).then_inc(consts_loaded, 16)
            sp.dma_start(strips_sb[:], strips).then_inc(consts_loaded, 16)
            for half in range(HALVES):
                sp.dma_start(z_cols[:, half, :, COL_PAIRS:],
                             dense[half * HB:(half + 1) * HB].rearrange("(t p) d -> p t d", p=P)
                             ).then_inc(dense_loaded, 16)
            full = K_ROWS // P
            mlp_loads = [
                (w1_sb[:, 0:full, :], w1[0:full * P].rearrange("(t p) n -> p t n", p=P)),
                (w1_sb[0:K_ROWS - full * P, full, :], w1[full * P:K_ROWS]),
                (w2_sb[:], w2.rearrange("(t p) n -> p t n", p=P)),
                (w3_sb[:], w3), (b1_sb[:], b1), (b2_sb[:], b2),
            ]
            for s in range(PIECES):
                sp.wait_ge(w_hi_ready, s + 1)
                sp.wait_ge(w_lo_ready, s + 1)
                for q in range(PER):
                    cols = slice(s * PIECE + q * QUARTER, s * PIECE + (q + 1) * QUARTER)
                    for r in range(PER):
                        part = w_hi[:].bitcast(F32) if r < 2 else w_raw[:]
                        sp.dma_start(w_stack[EMB * r:EMB * r + EMB, cols].bitcast(F32),
                                     part[EMB * q:EMB * q + EMB, s % 2, :]
                                     ).then_inc(w_stacked[s % 2], 16)
                if 1 <= s < PIECES - 1:
                    load_piece(s + 1)
                if s == 3:
                    for dst, src in mlp_loads:
                        sp.dma_start(dst, src).then_inc(mlp_loaded, 16)
            for half in range(HALVES):
                sp.wait_ge(side_drained, SIDE["mlp", half, MLP_Y] + 1)
                sp.dma_start(out[half * HB:(half + 1) * HB].rearrange("b o -> o b"), y_sb[:, half, :]
                             ).then_inc(stored, 16)
            sp.wait_ge(stored, 16 * HALVES)

        @block.gpsimd
        def _(pool):
            pool.wait_ge(ids_loaded, 16)
            for half in range(HALVES):
                for f in range(FIELDS):
                    g = f // PER
                    if half > 0 and f % PER == 0:
                        pool.wait_ge(gathered[g], 16 * PER * BT * half)
                    for t in range(BT):
                        row = ids_sb[:, half * BT + t, f:f + 1].bitcast(U32)
                        pool.indirect_dma_start(
                            x[:, half, t, EMB * f:EMB * f + EMB], None, tables[f],
                            bass.IndirectOffsetOnAxis(row, 0)).then_inc(gathered[g], 16)

        @block.scalar
        def _(act):
            def w_hi_part(s):
                act.wait_ge(w_loaded[s % 2], 16 * (s // 2 + 1))
                if s >= 2:
                    act.wait_ge(w_stacked[s % 2], 16 * PER * PER * (s // 2))
                act.copy(w_hi[:, s % 2, :], w_raw[:, s % 2, :]).then_inc(w_hi_ready, 1)

            def x_hi_part(gg):
                half, g = divmod(gg, GROUPS)
                act.wait_ge(gathered[g], 16 * PER * BT * (half + 1))
                if gg >= 2:
                    act.wait_ge(side_filled, last_job_of_group(gg - 2) + 1)
                group = x[:, half, :, P * g:P * g + P].rearrange("p t (k e) -> p t k e", k=PER)
                for t in range(BT):
                    last = act.copy(x_parts[:, gg % 2, t, :, 0:4:2, :],
                                    group[:, t].unsqueeze(2).to_broadcast([P, PER, 2, EMB]))
                last.then_inc(x_hi_ready, 1)

            def x_lo_again(gg):
                act.wait_ge(x_lo_ready, gg + 1)
                act.copy(x_parts[:, gg % 2, :, :, 3, :], x_parts[:, gg % 2, :, :, 1, :]
                         ).then_inc(x_parts_ready, 1)

            def drain_side(job):
                k = SIDE[job]
                act.wait_ge(side_filled, k + 1)
                src = side_ps[:, k % 2, 0:HB]
                if job[0] == "stack":
                    wait_count(act, t_filled, units_until(job[1] - STACK_SLOTS))
                    act.copy(x_stack[:, job[1] % STACK_SLOTS, :], src).then_inc(side_drained, 1)
                elif job[0] == "turn":
                    half, g = divmod(job[1], GROUPS)
                    act.copy(x_turned[:, half, g, :], src).then_inc(side_drained, 1)
                else:
                    _, half, s = job
                    if s == 0:
                        act.wait_ge(mlp_loaded, 16 * 6)
                    if s in MLP_T:
                        rows = min(P, COL_K - P * s)
                        act.copy(z_t[0:rows, ROW_TILES + s, :], src[0:rows, :]
                                 ).then_inc(side_drained, 1)
                    elif s in MLP_H1:
                        n = s - MLP_H1[0]
                        act.activation(h1[:, n, :], src, ACT.Relu, bias=b1_sb[:, n:n + 1]
                                       ).then_inc(side_drained, 1)
                    elif s in MLP_H2:
                        n = s - MLP_H2[0]
                        act.activation(h2[:, n, :], src, ACT.Relu, bias=b2_sb[:, n:n + 1]
                                       ).then_inc(side_drained, 1)
                    else:
                        act.copy(y_sb[:, half, :], src[0:1, :]).then_inc(side_drained, 1)

            def drain_z(t):
                act.wait_ge(rows_summed, row_index[last_row_unit[t]] + 1)
                if t >= ROW_TILES:
                    act.wait_ge(side_filled, SIDE["mlp", t // ROW_TILES - 1, MLP_H1[-1]] + 1)
                act.copy(z_t[:, t % ROW_TILES, :], z_ps[:, t % 2, 0:HB]).then_inc(z_drained, 1)

            act.wait_ge(consts_loaded, 32)
            act.copy(eye_r[:], eye_sb[:]).then_inc(eye_ready, 1)
            for n in range(STEPS + 1):
                for s in pieces_at(n):
                    w_hi_part(s)
                for gg in split_at(n):
                    x_hi_part(gg)
                for t in z_tiles_at(n):
                    drain_z(t)
                for job in side_jobs_at(n):
                    if job[0] == "stack" and job[1] % PER == 0:
                        x_lo_again(job[1] // PER)
                    drain_side(job)

        @block.tensor
        def _(pe):
            def fill_side(job):
                k = SIDE[job]
                dst = side_ps[:, k % 2, 0:HB]
                wait_count(pe, side_drained, k - 1)
                if job[0] == "stack":
                    gg = job[1] // PER
                    pe.wait_ge(x_parts_ready, gg + 1)
                    for t in range(BT):
                        part = x_parts[:, gg % 2, t, job[1] % PER, :, :].rearrange("p s e -> p (s e)")
                        mm = pe.matmul(dst[:, P * t:P * t + P], part, eye_r[:], start=True, stop=True)
                elif job[0] == "turn":
                    half, g = divmod(job[1], GROUPS)
                    pe.wait_ge(gathered[g], 16 * PER * BT * (half + 1))
                    for t in range(BT):
                        mm = pe.matmul(dst[:, P * t:P * t + P], x[:, half, t, P * g:P * g + P],
                                       eye_sb[:], start=True, stop=True)
                else:
                    _, half, s = job
                    if s == 0:
                        pe.wait_ge(cols_summed, (half + 1) * len(col_units) // HALVES)
                        pe.wait_ge(dense_loaded, 16 * HALVES)
                    else:
                        pe.wait_ge(side_drained, k)
                    if s in MLP_T:
                        rows = min(P, COL_K - P * s)
                        for t in range(BT):
                            mm = pe.matmul(dst[0:rows, P * t:P * t + P],
                                           z_cols[:, half, t, P * s:P * s + rows], eye_sb[:],
                                           start=True, stop=True)
                    elif s in MLP_H1:
                        n = s - MLP_H1[0]
                        if n == 0:
                            pe.wait_ge(z_drained, ROW_TILES * (half + 1))
                            pe.wait_ge(mlp_loaded, 16 * 6)
                        for t in range(K_TILES):
                            rows = min(P, K_ROWS - P * t)
                            mm = pe.matmul(dst, w1_sb[0:rows, t, P * n:P * n + P], z_t[0:rows, t, :],
                                           start=(t == 0), stop=(t == K_TILES - 1))
                    elif s in MLP_H2:
                        n = s - MLP_H2[0]
                        for t in range(HID1 // P):
                            mm = pe.matmul(dst, w2_sb[:, t, P * n:P * n + P], h1[:, t, :],
                                           start=(t == 0), stop=(t == HID1 // P - 1))
                    else:
                        for t in range(HID2 // P):
                            mm = pe.matmul(dst[0:1, :], w3_sb[:, t:t + 1], h2[:, t, :],
                                           start=(t == 0), stop=(t == HID2 // P - 1))
                mm.then_inc(side_filled, 1)

            def fill_t(n, u):
                i = n % FIELDS
                kind, a, b = UNITS[u % N_UNITS]
                stack = x_stack[:, n % STACK_SLOTS, :]
                wait_count(pe, multiplied, u - T_SLOTS + 1)
                if kind == "rows":
                    for c in range(b - a):
                        at = w_at(i) + P * (a + c)
                        mm = pe.matmul(t_ps[:, u % T_SLOTS, c // 2, HB * (c % 2):HB * (c % 2) + HB],
                                       w_stack[:, at:at + P], stack, start=True, stop=True)
                else:
                    for t in range(BT):
                        mm = pe.matmul(t_ps[:, u % T_SLOTS, t, 0:EMB * (b - a)],
                                       stack[:, P * t:P * t + P],
                                       w_stack[:, w_at(i) + EMB * a:w_at(i) + EMB * b],
                                       start=True, stop=True)
                mm.then_inc(t_filled, 1)

            def sum_rows(u):
                _, a, b = UNITS[u % N_UNITS]
                pe.wait_ge(multiplied, u + 1)
                for c in range(b - a):
                    m = first_chunk[u] + c
                    tile, strip, slot = m // 32, m % 4, m % 32 // 4
                    if m % 32 == 0:
                        wait_count(pe, z_drained, tile - 1)
                    mm = pe.matmul(z_ps[EMB * strip:EMB * strip + EMB, tile % 2, 0:HB],
                                   strips_sb[:, EMB - PER - PER * slot:2 * EMB - PER - PER * slot],
                                   row_prod[:, row_index[u] % ROW_SLOTS, c, :],
                                   start=(slot == 0), stop=(slot == 7), skip_group_check=True,
                                   tile_position=(0, EMB * strip))
                mm.then_inc(rows_summed, 1)

            pe.wait_ge(eye_ready, 1)
            for n in range(STEPS + 1):
                if n == STEPS:
                    for u in row_units:
                        if u not in sum_step:
                            sum_rows(u)
                for job in side_jobs_at(n):
                    fill_side(job)
                if n == STEPS:
                    break
                if n < FIELDS and n > 0:
                    wait_w_columns(pe, w_at(n + 1))
                for k, u in enumerate(units_at(n)):
                    if k == 0:
                        pe.wait_ge(side_drained, SIDE["stack", n] + 1)
                    fill_t(n, u)
                    for v in sums_after(u):
                        sum_rows(v)

        @block.vector
        def _(dve):
            def w_lo_part(s):
                dve.wait_ge(w_hi_ready, s + 1)
                dve.tensor_tensor(w_raw[:, s % 2, :], w_raw[:, s % 2, :], w_hi[:, s % 2, :],
                                  ALU.subtract).then_inc(w_lo_ready, 1)

            def x_lo_part(gg):
                half, g = divmod(gg, GROUPS)
                dve.wait_ge(x_hi_ready, gg + 1)
                if gg >= 2:
                    dve.wait_ge(side_filled, last_job_of_group(gg - 2) + 1)
                dve.wait_ge(gathered[g], 16 * PER * BT * (half + 1))
                group = x[:, half, :, P * g:P * g + P].rearrange("p t (k e) -> p t k e", k=PER)
                dve.tensor_tensor(x_parts[:, gg % 2, :, :, 1, :], group, x_parts[:, gg % 2, :, :, 0, :],
                                  ALU.subtract).then_inc(x_lo_ready, 1)

            def multiply(u):
                half = u // N_UNITS
                kind, a, b = UNITS[u % N_UNITS]
                dve.wait_ge(t_filled, u + 1)
                if kind == "rows":
                    slot = row_index[u] % ROW_SLOTS
                    dve.wait_ge(side_drained, SIDE["turn", half * GROUPS + b - 1] + 1)
                    wait_count(dve, rows_summed, row_index[u] - ROW_SLOTS + 1)
                    t = t_ps[:, u % T_SLOTS, :, :].rearrange("p k (c b) -> p (k c) b", b=HB)
                    dve.tensor_tensor(row_prod[:, slot, 0:b - a, :], t[:, 0:b - a, :],
                                      x_turned[:, half, a:b, :], ALU.mult).then_inc(multiplied, 1)
                else:
                    k = col_index[u]
                    wait_count(dve, cols_summed, k - COL_SLOTS + 1)
                    width = EMB * (b - a)
                    dve.tensor_tensor(col_prod[:, k % COL_SLOTS, :, 0:width],
                                      t_ps[:, u % T_SLOTS, :, 0:width],
                                      x[:, half, :, EMB * a:EMB * b], ALU.mult).then_inc(multiplied, 1)

            def sum_cols(u):
                half = u // N_UNITS
                _, a, b = UNITS[u % N_UNITS]
                k, at = col_index[u], col_at[u % N_UNITS]
                dve.wait_ge(multiplied, u + 1)
                prod = col_prod[:, k % COL_SLOTS, :, 0:EMB * (b - a)].rearrange(
                    "p t (j f) -> p t j f", f=EMB)
                dve.tensor_reduce(z_cols[:, half, :, at:at + b - a], prod, AX_X, ALU.add
                                  ).then_inc(cols_summed, 1)

            for n in range(STEPS):
                for s in pieces_at(n):
                    w_lo_part(s)
                for gg in split_at(n):
                    x_lo_part(gg)
                units = list(units_at(n))
                for u in units[:2]:
                    multiply(u)
                if units:
                    sum_cols(units[0])
                for u in units[2:]:
                    multiply(u)


def kernel(**inputs):
    import concourse.bacc as bacc
    from concourse.bass_utils import run_bass_kernel_spmd

    a = {name: np.ascontiguousarray(value) for name, value in inputs.items()}
    order = pair_order()
    index = {}
    for j in range(FIELDS):
        for i in range(j + 1, FIELDS):
            index[j, i] = len(index)
    by_field = [index[j, i] for i in range(FIELDS) for j in range(i)]
    w = a["L0_rec_W"][by_field].transpose(2, 0, 1).reshape(EMB, PIECES, PER, QUARTER)
    w_pieces = w.transpose(1, 2, 0, 3).reshape(PIECES, P, QUARTER)
    w1_rows = [index[p] for p in order] + list(range(PAIRS, PAIRS + DENSE))
    strips = np.zeros((P, 2 * EMB - PER), np.float32)
    for p in range(P):
        strips[p, EMB - PER + p // EMB] = 1.0
    laid = {
        "ids": a["ids"], **{f"tbl_{f}": a[f"tbl_{f}"] for f in range(FIELDS)},
        "dense": a["dense_ctx"], "w_pieces": w_pieces, "w1": a["W_top1"][w1_rows],
        "b1": a["b_top1"].reshape(HID1 // P, P).T, "w2": a["W_top2"],
        "b2": a["b_top2"].reshape(HID2 // P, P).T, "w3": a["W_top3"].reshape(HID2 // P, P).T,
        "eye": np.eye(P, dtype=np.float32), "strips": strips,
    }
    nc = bacc.Bacc("TRN2", target_bir_lowering=False, num_devices=1)
    arrays, ap = {}, {}
    for name, value in laid.items():
        value = np.ascontiguousarray(value)
        arrays[f"{name}_dram"] = value
        ap[name] = nc.dram_tensor(f"{name}_dram", value.shape, mybir.dt.from_np(value.dtype),
                                  kind="ExternalInput").ap()
    out = nc.dram_tensor("y_dram", (BATCH, 1), F32, kind="ExternalOutput").ap()
    program(nc, ap["ids"], [ap[f"tbl_{f}"] for f in range(FIELDS)], ap["dense"], ap["w_pieces"],
            ap["w1"], ap["b1"], ap["w2"], ap["b2"], ap["w3"], ap["eye"], ap["strips"], out)
    got = run_bass_kernel_spmd(nc, [arrays], core_ids=[0])
    return got.results[0]["y_dram"]
```

```python
from contextlib import ExitStack

import numpy as np

import concourse.bass as bass
from concourse import mybir

F32 = mybir.dt.float32
F32R = mybir.dt.float32r
I32 = mybir.dt.int32
U32 = mybir.dt.uint32
ALU = mybir.AluOpType
ACT = mybir.ActivationFunctionType
AX_X = mybir.AxisListType.X

P = 128
BATCH, FIELDS, EMB, DENSE = 512, 40, 32, 16
HID1, HID2 = 512, 256
BANK = 512
PER = P // EMB
GROUPS = FIELDS // PER
TILES = BATCH // P
PARTS = [(0, 2), (2, 1), (3, 1)]
STEPS = len(PARTS) * GROUPS

COLS = [0, 0, 0, 0, 0, 1, 1, 1, 1, 1]
ROWS = [g - COLS[g] for g in range(GROUPS)]
PAIRS = FIELDS * (FIELDS - 1) // 2
DIAG = [(2, 0), (2, 1), (3, 0), (3, 1), (1, 0), (3, 2)]
CHUNKS = PER * sum(ROWS)
ROW_TILES = -(-CHUNKS // 32)
COL_PAIRS = PAIRS - CHUNKS * PER
COL_K = COL_PAIRS + DENSE
COL_TILES = -(-COL_K // P)
K_TILES = ROW_TILES + COL_TILES
assert CHUNKS % 32 == 0

W_COLS = PAIRS * EMB
PIECES = 13
PIECE = W_COLS // PIECES
QUARTER = PIECE // PER
assert QUARTER * PER * PIECES == W_COLS and QUARTER <= BANK

T_SLOTS, PROD_SLOTS, RAW_SLOTS = 2, 3, 3
UNIT = 2 * BANK


def w_at(g, other=None):
    base = sum(PER * P * k + len(DIAG) * EMB for k in range(g))
    return base + PER * P * (g if other is None else other)


def units_of(k):
    part, g = divmod(k, GROUPS)
    wide = UNIT // (PER * P * PARTS[part][1])
    return ([("diag", k, g, g)] + [("cols", k, a, a + 1) for a in range(ROWS[g], g)]
            + [("rows", k, a, min(a + wide, ROWS[g])) for a in range(0, ROWS[g], wide)])


UNITS = [u for k in range(STEPS) for u in units_of(k)]
FIRST_UNIT = [sum(len(units_of(j)) for j in range(k)) for k in range(STEPS + 1)]


def chunk_of(k, other):
    part, g = divmod(k, GROUPS)
    return part * CHUNKS + PER * (sum(ROWS[:g]) + other)


def z_row(m):
    return m // 32 * P + m % 4 * 32 + m % 32 // 4 * PER


def z_col(g, kind):
    base = sum(len(DIAG) + PER * PER * COLS[h] for h in range(g))
    return base + (len(DIAG) if kind == "cols" else 0)


def pair_order():
    rows, cols = [None] * (CHUNKS * PER), []
    for g in range(GROUPS):
        for a in range(ROWS[g]):
            for r in range(PER):
                for s in range(PER):
                    rows[z_row(chunk_of(g, a) + r) + s] = (PER * a + s, PER * g + r)
        cols += [(PER * g + j, PER * g + i) for i, j in DIAG]
        for a in range(ROWS[g], g):
            cols += [(PER * a + s, PER * g + r) for r in range(PER) for s in range(PER)]
    return rows + cols


def sums_until(k, other):
    return chunk_of(k, other) // PER + 1


def mlp_stages(tile):
    return ([("z_turn", tile, s) for s in range(COL_TILES)]
            + [("h1", tile, t) for t in range(K_TILES)]
            + [("h2", tile), ("y", tile)])


def make_plan():
    plan = [("w_split", 0)]
    for s in range(PIECES):
        plan += [("w_split", s + 1)] * (s + 1 < PIECES) + [("w_spread", s, q) for q in range(PER)]

    def prepare(k):
        tiles = PARTS[k // GROUPS][1]
        turn = [("turn", k)] if k % GROUPS < GROUPS - 1 else []
        return [("stack", k, j) for j in range(tiles)] + turn

    def sums(u):
        if u < 0 or UNITS[u][0] != "rows":
            return []
        _, k, a, b = UNITS[u]
        stages = []
        for other in range(a, b):
            stages.append(("sum", u, other))
            if chunk_of(k, other) % 32 == 32 - PER:
                stages.append(("z_out", chunk_of(k, other) // 32))
        return stages

    mlp = []
    plan += [("split", 0)] + prepare(0)
    for k in range(STEPS):
        part, g = divmod(k, GROUPS)
        if g == 1 and part > 0:
            first, tiles = PARTS[part - 1]
            mlp += [stage for t in range(first, first + tiles) for stage in mlp_stages(t)]
        mine = list(range(FIRST_UNIT[k], FIRST_UNIT[k + 1]))
        for u in mine:
            if k + 1 < STEPS and u == mine[max(0, len(mine) - 3)]:
                plan.append(("split", k + 1))
            if k + 1 < STEPS and u == mine[-1]:
                plan += prepare(k + 1)
            plan += [("unit", u)] + sums(u - 2)
            if mlp:
                plan.append(mlp.pop(0))
    plan += sums(len(UNITS) - 2) + sums(len(UNITS) - 1) + mlp
    return plan + mlp_stages(PARTS[-1][0])


PLAN = make_plan()


def numbered(*kinds):
    return {stage: n for n, stage in enumerate(s for s in PLAN if s[0] in kinds)}


SIDE = numbered("stack", "turn", "z_turn")
COL_UNITS = [u for u, unit in enumerate(UNITS) if unit[0] != "rows"]
COL_INDEX = {u: n for n, u in enumerate(COL_UNITS)}


def program(nc, ids, tables, dense, w_pieces, w1, b1, w2, b2, w3, eye, strips, spread, out):
    with ExitStack() as ctx:
        def sb(name, shape, dt=F32, stack=ctx):
            return stack.enter_context(nc.sbuf_tensor(name, shape, dt))

        def psum(name, shape):
            return ctx.enter_context(nc.psum_tensor(name, shape, F32))

        def sem(name):
            return ctx.enter_context(nc.semaphore(name))

        ids_sb = sb("ids_sb", [P, TILES, FIELDS], I32)
        x = sb("x", [P, TILES, FIELDS * EMB])
        x_parts = sb("x_parts", [P, 2, PER, 4, EMB], F32R)
        x_stack = sb("x_stack", [P, 2, UNIT], F32R)
        x_turned = sb("x_turned", [P, GROUPS - 1, BATCH])
        w_stack = sb("w_stack", [P, W_COLS], F32R)
        prod = sb("prod", [P, PROD_SLOTS, UNIT])
        z_cols = sb("z_cols", [P, TILES, COL_K])
        z_t = sb("z_t", [P, K_TILES, BATCH])
        w2_sb = sb("w2_sb", [P, HID1 // P, HID2])
        w3_sb = sb("w3_sb", [P, HID2 // P])
        b1_sb = sb("b1_sb", [P, HID1 // P])
        b2_sb = sb("b2_sb", [P, HID2 // P])
        h1 = sb("h1", [P, HID1 // P, P])
        h2 = sb("h2", [P, HID2 // P, P])
        y_sb = sb("y_sb", [1, TILES, P])
        eye_sb = sb("eye_sb", [P, P])
        eye_r = sb("eye_r", [P, P], F32R)
        strips_sb = sb("strips_sb", [P, 2 * EMB - PER])
        with ExitStack() as early:
            spread_sb = sb("spread_sb", [P, PER * 6 * EMB // 4, 4], stack=early)
            spread_r = sb("spread_r", [P, PER, 6 * EMB], F32R, early)
            w_raw = sb("w_raw", [P, RAW_SLOTS, QUARTER], F32, early)
            w_hi = sb("w_hi", [P, 2, QUARTER], F32R, early)
            w_lo = sb("w_lo", [P, 2, QUARTER], F32R, early)
        w1_sb = sb("w1_sb", [P, K_TILES, HID1])

        t_ps = psum("t_ps", [P, T_SLOTS, UNIT])
        side_ps = psum("side_ps", [P, 2, BANK])
        z_ps = psum("z_ps", [P, BANK])
        mlp_ps = psum("mlp_ps", [P, PER, P])

        ids_loaded = sem("ids_loaded")
        dense_loaded = sem("dense_loaded")
        consts_loaded = sem("consts_loaded")
        mlp_loaded = sem("mlp_loaded")
        gathered = [sem(f"gathered_{g}") for g in range(GROUPS)]
        w_loaded = [sem(f"w_loaded_{s}") for s in range(RAW_SLOTS)]
        w_hi_ready = sem("w_hi_ready")
        w_lo_ready = sem("w_lo_ready")
        w_spread = sem("w_spread")
        w_stacked_act = sem("w_stacked_act")
        w_stacked_dve = sem("w_stacked_dve")
        consts_ready = sem("consts_ready")
        x_hi_ready = sem("x_hi_ready")
        x_lo_ready = sem("x_lo_ready")
        x_parts_ready = sem("x_parts_ready")
        side_filled = sem("side_filled")
        side_drained = sem("side_drained")
        t_filled = sem("t_filled")
        multiplied = sem("multiplied")
        cols_summed = sem("cols_summed")
        rows_summed = sem("rows_summed")
        z_drained = sem("z_drained")
        mlp_filled = sem("mlp_filled")
        mlp_drained = sem("mlp_drained")
        stored = sem("stored")

        def gathers_until(part):
            return 16 * PER * (PARTS[part][0] + PARTS[part][1])

        def batch_of(k):
            first, tiles = PARTS[k // GROUPS]
            return first, tiles, slice(P * first, P * (first + tiles))

        def stack_of(k):
            width = P * PARTS[k // GROUPS][1]
            return x_stack[:, k % 2, 0:PER * width].rearrange("p (r b) -> p r b", r=PER)

        block = ctx.enter_context(nc.Block())

        @block.sync
        def _(sp):
            sp.dma_start(ids_sb[:], ids.rearrange("(t p) f -> p t f", p=P)).then_inc(ids_loaded, 16)
            for s in range(PIECES):
                if s >= RAW_SLOTS:
                    sp.wait_ge(w_lo_ready, s - RAW_SLOTS + 1)
                sp.dma_start(w_raw[:, s % RAW_SLOTS, :], w_pieces[s]).then_inc(w_loaded[s % RAW_SLOTS], 16)
                if s == 1:
                    sp.dma_start(spread_sb[:].rearrange("p a b -> p (a b)"), spread).then_inc(consts_loaded, 16)
                    sp.dma_start(eye_sb[:], eye).then_inc(consts_loaded, 16)
                    sp.dma_start(strips_sb[:], strips).then_inc(consts_loaded, 16)
            sp.dma_start(z_cols[:, :, COL_PAIRS:], dense.rearrange("(t p) d -> p t d", p=P)
                         ).then_inc(dense_loaded, 16)
            sp.wait_ge(w_spread, PIECES * PER)
            full = (ROW_TILES * P + COL_K) // P
            rest = (ROW_TILES * P + COL_K) % P
            sp.dma_start(w1_sb[:, 0:full, :], w1[0:full * P].rearrange("(t p) n -> p t n", p=P)
                         ).then_inc(mlp_loaded, 16)
            sp.dma_start(w1_sb[0:rest, full, :], w1[full * P:]).then_inc(mlp_loaded, 16)
            sp.dma_start(w2_sb[:], w2.rearrange("(t p) n -> p t n", p=P)).then_inc(mlp_loaded, 16)
            sp.dma_start(w3_sb[:], w3).then_inc(mlp_loaded, 16)
            sp.dma_start(b1_sb[:], b1).then_inc(mlp_loaded, 16)
            sp.dma_start(b2_sb[:], b2).then_inc(mlp_loaded, 16)
            for t in range(TILES):
                sp.wait_ge(mlp_drained, 3 * (t + 1))
                sp.dma_start(out[P * t:P * t + P].rearrange("b o -> o b"), y_sb[:, t, :]
                             ).then_inc(stored, 16)
            sp.wait_ge(stored, 16 * TILES)

        @block.gpsimd
        def _(pool):
            pool.wait_ge(ids_loaded, 16)
            for part, (first, tiles) in enumerate(PARTS):
                for f in range(FIELDS):
                    g = f // PER
                    if part > 0 and f % PER == 0:
                        pool.wait_ge(gathered[g], gathers_until(part - 1))
                    for t in range(first, first + tiles):
                        pool.indirect_dma_start(
                            x[:, t, EMB * f:EMB * f + EMB], None, tables[f],
                            bass.IndirectOffsetOnAxis(ids_sb[:, t, f:f + 1].bitcast(U32), 0)
                        ).then_inc(gathered[g], 16)

        @block.scalar
        def _(act):
            act.wait_ge(consts_loaded, 48)
            act.copy(spread_r[:].rearrange("p q c -> p (q c)"), spread_sb[:].rearrange("p a b -> p (a b)")
                     ).then_inc(consts_ready, 1)
            act.copy(eye_r[:], eye_sb[:]).then_inc(consts_ready, 1)
            for stage in PLAN:
                kind, k = stage[0], stage[1]
                if kind == "w_split":
                    act.wait_ge(w_loaded[k % RAW_SLOTS], 16 * (k // RAW_SLOTS + 1))
                    if k >= 2:
                        act.wait_ge(w_spread, PER * (k - 1))
                    act.copy(w_hi[:, k % 2, :], w_raw[:, k % RAW_SLOTS, :]).then_inc(w_hi_ready, 1)
                elif kind == "w_spread" and stage[2] < 2:
                    q = stage[2]
                    act.wait_ge(w_spread, PER * k + q + 1)
                    at = k * PIECE + q * QUARTER
                    act.copy(w_stack[:, at:at + QUARTER], t_ps[:, 0, BANK * q:BANK * q + QUARTER]
                             ).then_inc(w_stacked_act, 1)
                elif kind == "split":
                    part, g = divmod(k, GROUPS)
                    first, tiles, _ = batch_of(k)
                    act.wait_ge(gathered[g], gathers_until(part))
                    if k > 0:
                        act.wait_ge(side_filled, SIDE["stack", k - 1, PARTS[(k - 1) // GROUPS][1] - 1] + 1)
                    for t in range(tiles):
                        group = x[:, first + t, P * g:P * g + P].rearrange("p (r e) -> p r e", r=PER)
                        last = act.copy(x_parts[:, t, :, 0:4:2, :],
                                        group.unsqueeze(2).to_broadcast([P, PER, 2, EMB]))
                    last.then_inc(x_hi_ready, 1)
                elif kind == "stack":
                    tiles, job = PARTS[k // GROUPS][1], stage[2]
                    if job == 0:
                        act.wait_ge(x_lo_ready, k + 1)
                        act.copy(x_parts[:, 0:tiles, :, 3, :], x_parts[:, 0:tiles, :, 1, :]
                                 ).then_inc(x_parts_ready, 1)
                    n = SIDE[stage]
                    act.wait_ge(side_filled, n + 1)
                    if k >= 2:
                        act.wait_ge(t_filled, FIRST_UNIT[k - 1])
                    act.copy(x_stack[:, k % 2, BANK * job:BANK * job + BANK], side_ps[:, n % 2, :]
                             ).then_inc(side_drained, 1)
                elif kind == "turn":
                    n, (_, tiles, rows) = SIDE[stage], batch_of(k)
                    act.wait_ge(side_filled, n + 1)
                    act.copy(x_turned[:, k % GROUPS, rows], side_ps[:, n % 2, 0:P * tiles]
                             ).then_inc(side_drained, 1)
                elif kind == "z_turn":
                    n, s = SIDE[stage], stage[2]
                    height = min(P, COL_K - P * s)
                    act.wait_ge(side_filled, n + 1)
                    act.copy(z_t[0:height, ROW_TILES + s, P * k:P * k + P], side_ps[0:height, n % 2, 0:P]
                             ).then_inc(side_drained, 1)
                elif kind == "z_out":
                    part, tile = divmod(k, ROW_TILES)
                    first, tiles = PARTS[part]
                    act.wait_ge(rows_summed, 32 // PER * (k + 1))
                    act.copy(z_t[:, tile, P * first:P * (first + tiles)], z_ps[:, 0:P * tiles]
                             ).then_inc(z_drained, 1)
                elif kind == "h1" and stage[2] == K_TILES - 1:
                    act.wait_ge(mlp_loaded, 16 * 6)
                    act.wait_ge(mlp_filled, 3 * k + 1)
                    for n in range(HID1 // P):
                        last = act.activation(h1[:, n, :], mlp_ps[:, n, :], ACT.Relu, bias=b1_sb[:, n:n + 1])
                    last.then_inc(mlp_drained, 1)
                elif kind == "h2":
                    act.wait_ge(mlp_filled, 3 * k + 2)
                    for n in range(HID2 // P):
                        last = act.activation(h2[:, n, :], mlp_ps[:, n, :], ACT.Relu, bias=b2_sb[:, n:n + 1])
                    last.then_inc(mlp_drained, 1)
                elif kind == "y":
                    act.wait_ge(mlp_filled, 3 * k + 3)
                    act.copy(y_sb[:, k, :], mlp_ps[0:1, 0, :]).then_inc(mlp_drained, 1)

        @block.tensor
        def _(pe):
            pe.wait_ge(consts_ready, 2)
            for stage in PLAN:
                kind, k = stage[0], stage[1]
                if kind == "w_spread":
                    q = stage[2]
                    pe.wait_ge(w_hi_ready, k + 1)
                    pe.wait_ge(w_lo_ready, k + 1)
                    if k >= 1:
                        pe.wait_ge(w_stacked_act if q < 2 else w_stacked_dve, 2 * (k - 1) + q % 2 + 1)
                    dst = t_ps[:, q // 2, BANK * (q % 2):BANK * (q % 2) + QUARTER]
                    pe.matmul(dst, spread_r[:, q, 2 * EMB:], w_hi[:, k % 2, :], start=True, stop=False)
                    pe.matmul(dst, spread_r[:, q, 0:4 * EMB], w_lo[:, k % 2, :], start=False, stop=True
                              ).then_inc(w_spread, 1)
                elif kind == "stack":
                    tiles, n = PARTS[k // GROUPS][1], SIDE[stage]
                    pe.wait_ge(x_parts_ready, k + 1)
                    if n >= 2:
                        pe.wait_ge(side_drained, n - 1)
                    for c in range(PER):
                        r, t = divmod(PER * stage[2] + c, tiles)
                        mm = pe.matmul(side_ps[:, n % 2, P * c:P * c + P],
                                       x_parts[:, t, r, :, :].rearrange("p s e -> p (s e)"), eye_r[:],
                                       start=True, stop=True)
                    mm.then_inc(side_filled, 1)
                elif kind == "turn":
                    n, (first, tiles, _) = SIDE[stage], batch_of(k)
                    g = k % GROUPS
                    pe.wait_ge(gathered[g], gathers_until(k // GROUPS))
                    if n >= 2:
                        pe.wait_ge(side_drained, n - 1)
                    for t in range(tiles):
                        mm = pe.matmul(side_ps[:, n % 2, P * t:P * t + P], x[:, first + t, P * g:P * g + P],
                                       eye_sb[:], start=True, stop=True)
                    mm.then_inc(side_filled, 1)
                elif kind == "unit":
                    what, step, a, b = UNITS[k]
                    g, (_, tiles, _) = step % GROUPS, batch_of(step)
                    width, stack = P * tiles, stack_of(step)
                    if k == 0:
                        pe.wait_ge(w_stacked_act, 2 * PIECES)
                        pe.wait_ge(w_stacked_dve, 2 * PIECES)
                    if k == FIRST_UNIT[step]:
                        pe.wait_ge(side_drained, SIDE["stack", step, tiles - 1] + 1)
                    if k >= T_SLOTS:
                        pe.wait_ge(multiplied, k - T_SLOTS + 1)
                    dst = t_ps[:, k % T_SLOTS, :]
                    if what == "rows":
                        for c in range(PER * (b - a)):
                            at = w_at(g, a) + P * c
                            mm = pe.matmul(dst[:, width * c:width * c + width], w_stack[:, at:at + P],
                                           stack[:, c % PER, :], start=True, stop=True)
                    elif what == "cols":
                        for t in range(tiles):
                            for r in range(PER):
                                at = w_at(g, a) + P * r
                                mm = pe.matmul(dst[:, BANK * t + P * r:BANK * t + P * r + P],
                                               stack[:, r, P * t:P * t + P], w_stack[:, at:at + P],
                                               start=True, stop=True)
                    else:
                        for t in range(tiles):
                            for r, c, n in ((2, 0, 2), (3, 2, 2), (1, 4, 1), (3, 5, 1)):
                                at, to = w_at(g) + EMB * c, BANK // 2 * t + EMB * c
                                mm = pe.matmul(dst[:, to:to + EMB * n], stack[:, r, P * t:P * t + P],
                                               w_stack[:, at:at + EMB * n], start=True, stop=True)
                    mm.then_inc(t_filled, 1)
                elif kind == "sum":
                    _, step, a, _ = UNITS[k]
                    other = stage[2]
                    width = P * batch_of(step)[1]
                    pe.wait_ge(multiplied, k + 1)
                    for c in range(PER):
                        m, at = chunk_of(step, other) + c, width * (PER * (other - a) + c)
                        strip, slot = m % 4, m % 32 // 4
                        if m % 32 == 0 and m > 0:
                            pe.wait_ge(z_drained, m // 32)
                        mm = pe.matmul(z_ps[EMB * strip:EMB * strip + EMB, 0:width],
                                       strips_sb[:, EMB - PER - PER * slot:2 * EMB - PER - PER * slot],
                                       prod[:, k % PROD_SLOTS, at:at + width],
                                       start=(slot == 0), stop=(slot == 7), skip_group_check=True,
                                       tile_position=(0, EMB * strip))
                    mm.then_inc(rows_summed, 1)
                elif kind == "z_turn":
                    n, s = SIDE[stage], stage[2]
                    height = min(P, COL_K - P * s)
                    if s == 0:
                        part = next(p for p, (first, tiles) in enumerate(PARTS) if k < first + tiles)
                        end = FIRST_UNIT[GROUPS * (part + 1)]
                        pe.wait_ge(cols_summed, sum(u < end for u in COL_UNITS))
                        pe.wait_ge(dense_loaded, 16)
                    pe.wait_ge(side_drained, n - 1)
                    pe.matmul(side_ps[0:height, n % 2, 0:P], z_cols[:, k, P * s:P * s + height],
                              eye_sb[:], start=True, stop=True).then_inc(side_filled, 1)
                elif kind == "h1":
                    t = stage[2]
                    height = min(P, COL_K - P * (t - ROW_TILES)) if t >= ROW_TILES else P
                    if t == 0:
                        pe.wait_ge(mlp_loaded, 16 * 6)
                        if k > 0:
                            pe.wait_ge(mlp_drained, 3 * k)
                    if t < ROW_TILES:
                        part = next(p for p, (first, tiles) in enumerate(PARTS) if k < first + tiles)
                        pe.wait_ge(z_drained, ROW_TILES * part + t + 1)
                    else:
                        pe.wait_ge(side_drained, SIDE["z_turn", k, t - ROW_TILES] + 1)
                    for n in range(HID1 // P):
                        mm = pe.matmul(mlp_ps[:, n, :], w1_sb[0:height, t, P * n:P * n + P],
                                       z_t[0:height, t, P * k:P * k + P], start=(t == 0 and n == 0),
                                       stop=(t == K_TILES - 1), skip_group_check=True)
                    if t == K_TILES - 1:
                        mm.then_inc(mlp_filled, 1)
                elif kind == "h2":
                    pe.wait_ge(mlp_drained, 3 * k + 1)
                    for n in range(HID2 // P):
                        for t in range(HID1 // P):
                            mm = pe.matmul(mlp_ps[:, n, :], w2_sb[:, t, P * n:P * n + P], h1[:, t, :],
                                           start=(t == 0), stop=(t == HID1 // P - 1))
                    mm.then_inc(mlp_filled, 1)
                elif kind == "y":
                    pe.wait_ge(mlp_drained, 3 * k + 2)
                    for t in range(HID2 // P):
                        mm = pe.matmul(mlp_ps[0:1, 0, :], w3_sb[:, t:t + 1], h2[:, t, :],
                                       start=(t == 0), stop=(t == HID2 // P - 1))
                    mm.then_inc(mlp_filled, 1)

        @block.vector
        def _(dve):
            def sum_unit(u):
                what, step, a, _ = UNITS[u]
                g, (first, tiles, _) = step % GROUPS, batch_of(step)
                pairs = len(DIAG) if what == "diag" else PER * PER
                each = BANK // 2 if what == "diag" else BANK
                src = prod[:, u % PROD_SLOTS, 0:each * tiles].rearrange(
                    "p (t c) -> p t c", t=tiles)[:, :, 0:EMB * pairs].rearrange("p t (k e) -> p t k e", e=EMB)
                at = z_col(g, what) + (PER * PER * (a - ROWS[g]) if what == "cols" else 0)
                dve.wait_ge(multiplied, u + 1)
                dve.tensor_reduce(z_cols[:, first:first + tiles, at:at + pairs], src, AX_X, ALU.add
                                  ).then_inc(cols_summed, 1)

            for stage in PLAN:
                kind, k = stage[0], stage[1]
                if kind == "w_split":
                    dve.wait_ge(w_hi_ready, k + 1)
                    if k >= 2:
                        dve.wait_ge(w_spread, PER * (k - 1))
                    dve.tensor_tensor(w_lo[:, k % 2, :], w_raw[:, k % RAW_SLOTS, :], w_hi[:, k % 2, :],
                                      ALU.subtract).then_inc(w_lo_ready, 1)
                elif kind == "w_spread" and stage[2] >= 2:
                    q = stage[2]
                    dve.wait_ge(w_spread, PER * k + q + 1)
                    at = k * PIECE + q * QUARTER
                    dve.tensor_copy(w_stack[:, at:at + QUARTER], t_ps[:, 1, BANK * (q - 2):BANK * (q - 2) + QUARTER]
                                    ).then_inc(w_stacked_dve, 1)
                elif kind == "split":
                    part, g = divmod(k, GROUPS)
                    first, tiles, _ = batch_of(k)
                    dve.wait_ge(gathered[g], gathers_until(part))
                    dve.wait_ge(x_hi_ready, k + 1)
                    group = x[:, first:first + tiles, P * g:P * g + P].rearrange("p t (r e) -> p t r e", r=PER)
                    dve.tensor_tensor(x_parts[:, 0:tiles, :, 1, :], group, x_parts[:, 0:tiles, :, 0, :],
                                      ALU.subtract).then_inc(x_lo_ready, 1)
                elif kind == "unit":
                    what, step, a, b = UNITS[k]
                    g, (first, tiles, rows) = step % GROUPS, batch_of(step)
                    width = P * tiles
                    if k >= PROD_SLOTS:
                        before = k - PROD_SLOTS
                        if UNITS[before][0] == "rows":
                            dve.wait_ge(rows_summed, sums_until(UNITS[before][1], UNITS[before][3] - 1))
                        else:
                            dve.wait_ge(cols_summed, COL_INDEX[before] + 1)
                    if what == "rows":
                        dve.wait_ge(side_drained, SIDE["turn", step - g + b - 1] + 1)
                    dve.wait_ge(t_filled, k + 1)
                    t_in, p_out = t_ps[:, k % T_SLOTS, :], prod[:, k % PROD_SLOTS, :]
                    if what == "rows":
                        def view(y):
                            return y[:, 0:PER * width * (b - a)].rearrange("p (g r b) -> p g r b", r=PER, b=width)
                        other = x_turned[:, a:b, rows].unsqueeze(2).to_broadcast([P, b - a, PER, width])
                        dve.tensor_tensor(view(p_out), view(t_in), other, ALU.mult).then_inc(multiplied, 1)
                    elif what == "cols":
                        def view(y):
                            return y[:, 0:BANK * tiles].rearrange("p (t r c) -> p t r c", t=tiles, r=PER)
                        other = x[:, first:first + tiles, P * a:P * a + P].unsqueeze(2).to_broadcast(
                            [P, tiles, PER, P])
                        dve.tensor_tensor(view(p_out), view(t_in), other, ALU.mult).then_inc(multiplied, 1)
                    else:
                        def view(y, c, n):
                            return y[:, 0:BANK // 2 * tiles].rearrange("p (t c) -> p t c", t=tiles)[
                                :, :, EMB * c:EMB * (c + 2 * n)].rearrange("p t (s c) -> p t s c", s=2)
                        mine = x[:, first:first + tiles, P * g:P * g + P]
                        both = mine[:, :, 0:2 * EMB].unsqueeze(2).to_broadcast([P, tiles, 2, 2 * EMB])
                        even = mine.rearrange("p t (s c) -> p t s c", s=2)[:, :, :, 0:EMB]
                        dve.tensor_tensor(view(p_out, 0, 2), view(t_in, 0, 2), both, ALU.mult)
                        dve.tensor_tensor(view(p_out, 4, 1), view(t_in, 4, 1), even, ALU.mult
                                          ).then_inc(multiplied, 1)
                    if k - 1 in COL_INDEX:
                        sum_unit(k - 1)
            assert len(UNITS) - 1 not in COL_INDEX


def kernel(**inputs):
    import concourse.bacc as bacc
    from concourse.bass_utils import run_bass_kernel_spmd

    a = {name: np.ascontiguousarray(value) for name, value in inputs.items()}
    index = {}
    for j in range(FIELDS):
        for i in range(j + 1, FIELDS):
            index[j, i] = len(index)
    blocks = []
    for g in range(GROUPS):
        blocks += [index[PER * o + s, PER * g + r] for o in range(g) for r in range(PER) for s in range(PER)]
        blocks += [index[PER * g + j, PER * g + i] for i, j in DIAG]
    w = a["L0_rec_W"][blocks].transpose(2, 0, 1).reshape(EMB, PIECES, PER, QUARTER)
    w_pieces = w.transpose(1, 2, 0, 3).reshape(PIECES, P, QUARTER)
    w1_rows = [index[p] for p in pair_order()] + list(range(PAIRS, PAIRS + DENSE))
    strips = np.zeros((P, 2 * EMB - PER), np.float32)
    spread = np.zeros((P, PER, 6 * EMB), np.float32)
    for p in range(P):
        strips[p, EMB - PER + p // EMB] = 1.0
        spread[p, p // EMB, 2 * EMB + p % EMB] = 1.0
        spread[p, p // EMB, 3 * EMB + p % EMB] = 1.0
    laid = {
        "ids": a["ids"], **{f"tbl_{f}": a[f"tbl_{f}"] for f in range(FIELDS)},
        "dense": a["dense_ctx"], "w_pieces": w_pieces, "w1": a["W_top1"][w1_rows],
        "b1": a["b_top1"].reshape(HID1 // P, P).T, "w2": a["W_top2"],
        "b2": a["b_top2"].reshape(HID2 // P, P).T, "w3": a["W_top3"].reshape(HID2 // P, P).T,
        "eye": np.eye(P, dtype=np.float32), "strips": strips, "spread": spread.reshape(P, -1),
    }
    nc = bacc.Bacc("TRN2", target_bir_lowering=False, num_devices=1)
    arrays, ap = {}, {}
    for name, value in laid.items():
        value = np.ascontiguousarray(value)
        arrays[f"{name}_dram"] = value
        ap[name] = nc.dram_tensor(f"{name}_dram", value.shape, mybir.dt.from_np(value.dtype),
                                  kind="ExternalInput").ap()
    out = nc.dram_tensor("y_dram", (BATCH, 1), F32, kind="ExternalOutput").ap()
    program(nc, ap["ids"], [ap[f"tbl_{f}"] for f in range(FIELDS)], ap["dense"], ap["w_pieces"],
            ap["w1"], ap["b1"], ap["w2"], ap["b2"], ap["w3"], ap["eye"], ap["strips"], ap["spread"], out)
    got = run_bass_kernel_spmd(nc, [arrays], core_ids=[0])
    return got.results[0]["y_dram"]
```

```python
from contextlib import ExitStack

import numpy as np

import concourse.bass as bass
from concourse import mybir

F32 = mybir.dt.float32
F32R = mybir.dt.float32r
I32 = mybir.dt.int32
U32 = mybir.dt.uint32
ALU = mybir.AluOpType
ACT = mybir.ActivationFunctionType
AX_X = mybir.AxisListType.X

P = 128
BATCH, FIELDS, EMB, DENSE = 512, 40, 32, 16
HID1, HID2 = 512, 256
BANK = 512
PER = P // EMB
GROUPS = FIELDS // PER
TILES = BATCH // P
PART_TILES = 2
PARTS = TILES // PART_TILES
ROWS_B = P * PART_TILES
STEPS = PARTS * GROUPS

PAIRS = FIELDS * (FIELDS - 1) // 2
DIAG = [(1, 0), (2, 0), (2, 1), (3, 0), (3, 1), (3, 2)]
CHUNKS = PER * sum(range(GROUPS))
ROW_TILES = -(-CHUNKS // 32)
DIAG_PAIRS = GROUPS * len(DIAG)
DIAG_K = DENSE + DIAG_PAIRS
assert CHUNKS * PER + DIAG_PAIRS == PAIRS and DIAG_K <= P
K_TILES = ROW_TILES + 1
H1_ORDER = [*range(ROW_TILES - 2), K_TILES - 1, ROW_TILES - 2, ROW_TILES - 1]

W_COLS = PAIRS * EMB
QUARTERS = [1040] * 6
PIECES = len(QUARTERS)
PIECE_AT = [PER * sum(QUARTERS[:n]) for n in range(PIECES + 1)]
assert PIECE_AT[-1] == W_COLS

T_SLOTS, PROD_SLOTS, RAW_SLOTS, STACK_SLOTS, PART_SLOTS = 3, 3, 2, 2, 2
UNIT = PER * ROWS_B
assert UNIT == 2 * BANK
PIECES_BEFORE = [2, 0, 1, 1, 0, 1, 1]
MLP_STEP, MLP_UNITS = 2, 2
SUM_LAG = 2
EARLY_Z, LATE_TURNED = 2, 2
STACK_LEAD, SPLIT_LEAD = 1, 4


def w_at(g, other=None):
    base = sum(PER * P * k + len(DIAG) * EMB for k in range(g))
    return base + PER * P * (g if other is None else other)


def units_of(k):
    g = k % GROUPS
    return [("diag", k, g)] + [("rows", k, a) for a in range(g)]


UNITS = [u for k in range(STEPS) for u in units_of(k)]
FIRST_UNIT = [sum(len(units_of(j)) for j in range(k)) for k in range(STEPS + 1)]


def chunk_of(k, other):
    return PER * (sum(range(k % GROUPS)) + other)


def completes(k, other):
    m = chunk_of(k, other) + PER
    return m % 32 == 0 or m == CHUNKS


def z_row(m):
    return m // 32 * P + m % 4 * 32 + m % 32 // 4 * PER


def z_at(g):
    return DENSE + len(DIAG) * g


def pair_order():
    rows, cols = [None] * (ROW_TILES * P), []
    for g in range(GROUPS):
        for a in range(g):
            for r in range(PER):
                for s in range(PER):
                    rows[z_row(chunk_of(g, a) + r) + s] = (PER * a + s, PER * g + r)
        cols += [(PER * g + j, PER * g + i) for i, j in DIAG]
    return rows, cols


def pieces_until(g):
    return next(n for n in range(PIECES + 1) if PIECE_AT[n] >= w_at(g + 1, 0))


def mlp_stages(tile):
    return [("h1", tile, t) for t in H1_ORDER] + [("relu1", tile), ("h2", tile), ("relu2", tile), ("y", tile)]


def make_plan():
    after = {u: [] for u in range(-1, len(UNITS))}

    stacks, splits = [], [-1]
    for k in range(1, STEPS):
        stack = max(FIRST_UNIT[k] - 1 - STACK_LEAD, FIRST_UNIT[max(k - STACK_SLOTS + 1, 0)] - 1)
        if stacks:
            stack = max(stack, stacks[-1])
        stacks.append(stack)
        split = max(stack - SPLIT_LEAD, stacks[-1 - PART_SLOTS] if len(stacks) > PART_SLOTS else -1)
        splits.append(max(split, splits[-1]))
        after[splits[-1]].append(("split", k))
        after[stack].append(("stack", k))
        if k % GROUPS < GROUPS - 1:
            after[min(stack + 1, FIRST_UNIT[k + 1] - 1)].append(("turn", k))
    sums = {}
    for u, (what, k, a) in enumerate(UNITS):
        if what == "rows":
            to = min(u + SUM_LAG, len(UNITS) - 1)
            sums.setdefault(to, []).append(("sum", u))
            if completes(k, a):
                sums[to].append(("z_out", k // GROUPS, chunk_of(k, a) // 32))
    first_tile = PART_TILES * (PARTS - 1)
    for part in range(PARTS - 1):
        due = [("z_turn", part)]
        for tile in range(PART_TILES * part, PART_TILES * (part + 1)):
            due += mlp_stages(tile)
        for n, stage in enumerate(due):
            after[FIRST_UNIT[GROUPS * (part + 1) + MLP_STEP] + MLP_UNITS * n].append(stage)
    early = [("z_turn", PARTS - 1)] + [("h1", first_tile, t) for t in H1_ORDER[:-2]]
    for n, stage in enumerate(early):
        after[FIRST_UNIT[STEPS - 1] + 2 + n].append(stage)
    tail = [("h1", t, c) for t in range(first_tile + 1, TILES) for c in H1_ORDER[:-1]]

    plan, pieces = [], 0

    def add(stages):
        nonlocal pieces
        for stage in stages:
            if stage[0] == "split" and stage[1] < len(PIECES_BEFORE):
                for _ in range(PIECES_BEFORE[stage[1]]):
                    plan.append(("w_split", pieces))
                    pieces += 1
            plan.append(stage)

    add([("split", 0), ("stack", 0), ("turn", 0)] + after[-1])
    for u in range(len(UNITS)):
        assert not (u in FIRST_UNIT[:GROUPS] and pieces < pieces_until(UNITS[u][1]))
        add([("unit", u)])
        if u < len(UNITS) - 1:
            add(sums.get(u, []))
        add(after[u])
    plan += tail[:2] + sums[len(UNITS) - 1] + tail[2:]
    plan += [("h1", first_tile, c) for c in H1_ORDER[-2:]]
    for t in range(first_tile + 1, TILES):
        plan.append(("h1", t, H1_ORDER[-1]))
    for kind in ("relu1", "h2", "relu2", "y"):
        plan += [(kind, t) for t in range(first_tile, TILES)]
    return plan


PLAN = make_plan()


def numbered(*kinds):
    return {stage: n for n, stage in enumerate(s for s in PLAN if s[0] in kinds)}


SIDE = numbered("stack", "turn", "z_turn")
T_JOBS = [s for s in PLAN if s[0] in ("unit", "stack", "turn", "z_turn")
          or s == ("h1", TILES - 1, H1_ORDER[0])]
T_INDEX = {stage: n for n, stage in enumerate(T_JOBS)}
SUM_INDEX = numbered("sum")
DIAG_UNITS = [u for u, unit in enumerate(UNITS) if unit[0] != "rows"]
DIAG_INDEX = {u: n for n, u in enumerate(DIAG_UNITS)}


def program(nc, ids, tables, dense, w, w1, b1, w2, b2, w3, eye, strips, out):
    with ExitStack() as ctx:
        def sb(name, shape, dt=F32, stack=ctx):
            return stack.enter_context(nc.sbuf_tensor(name, shape, dt))

        def psum(name, shape):
            return ctx.enter_context(nc.psum_tensor(name, shape, F32))

        def sem(name):
            return ctx.enter_context(nc.semaphore(name))

        ids_sb = sb("ids_sb", [P, TILES, FIELDS], I32)
        x = sb("x", [P, TILES, FIELDS * EMB])
        x_parts = sb("x_parts", [P, PART_SLOTS, PART_TILES, PER, 4, EMB], F32R)
        x_stack = sb("x_stack", [P, STACK_SLOTS, UNIT], F32R)
        x_turned = [sb(f"x_turned_{g}", [P, BATCH]) for g in range(GROUPS - 1 - LATE_TURNED)]
        w_stack = sb("w_stack", [P, W_COLS], F32R)
        prod = sb("prod", [P, PROD_SLOTS, UNIT])
        z_diag = sb("z_diag", [P, TILES, DIAG_K])
        z_t = [sb(f"z_t_{t}", [P, BATCH]) for t in range(EARLY_Z)]
        w2_sb = sb("w2_sb", [P, HID1 // P, HID2])
        w3_sb = sb("w3_sb", [P, HID2 // P])
        b1_sb = sb("b1_sb", [P, HID1 // P])
        b2_sb = sb("b2_sb", [P, HID2 // P])
        h1 = sb("h1", [P, 2, HID1 // P, P])
        h2 = sb("h2", [P, 2, HID2 // P, P])
        y_sb = sb("y_sb", [1, 2, P])
        eye_sb = sb("eye_sb", [P, P])
        eye_r = sb("eye_r", [P, P], F32R)
        strips_sb = sb("strips_sb", [P, 2 * EMB - PER])
        with ExitStack() as early:
            w_hi = sb("w_hi", [P, 2, max(QUARTERS)], F32R, early)
            w_raw_0 = sb("w_raw_0", [P, max(QUARTERS)], F32, early)
        z_t += [sb(f"z_t_{t}", [P, BATCH]) for t in range(EARLY_Z, K_TILES)]
        x_turned += [sb(f"x_turned_{g}", [P, BATCH]) for g in range(GROUPS - 1 - LATE_TURNED, GROUPS - 1)]
        with ExitStack() as early:
            w_raw_1 = sb("w_raw_1", [P, max(QUARTERS)], F32, early)
            w_lo = sb("w_lo", [P, 2, max(QUARTERS)], F32R, early)
        w_raw = [w_raw_0, w_raw_1]
        w1_sb = sb("w1_sb", [P, K_TILES, HID1])

        t_ps = psum("t_ps", [P, T_SLOTS, UNIT])
        z_ps = psum("z_ps", [P, BANK])
        mlp_ps = psum("mlp_ps", [P, BANK])

        ids_loaded = sem("ids_loaded")
        dense_loaded = sem("dense_loaded")
        consts_loaded = sem("consts_loaded")
        mlp_loaded = sem("mlp_loaded")
        gathered = [sem(f"gathered_{g}") for g in range(GROUPS)]
        w_loaded = [sem(f"w_loaded_{s}") for s in range(RAW_SLOTS)]
        w_hi_ready = sem("w_hi_ready")
        w_lo_ready = sem("w_lo_ready")
        w_stacked = [sem(f"w_stacked_{s}") for s in range(PIECES)]
        consts_ready = sem("consts_ready")
        x_hi_ready = sem("x_hi_ready")
        x_lo_ready = sem("x_lo_ready")
        x_parts_ready = sem("x_parts_ready")
        side_filled = sem("side_filled")
        side_drained = sem("side_drained")
        t_filled = sem("t_filled")
        multiplied = sem("multiplied")
        diag_summed = sem("diag_summed")
        rows_summed = sem("rows_summed")
        z_drained = sem("z_drained")
        h1_filled = sem("h1_filled")
        h2_filled = sem("h2_filled")
        y_filled = sem("y_filled")
        h1_ready = sem("h1_ready")
        h2_ready = sem("h2_ready")
        y_ready = sem("y_ready")
        stored = [sem(f"stored_{s}") for s in range(2)]

        W_COPIES = 16 * PER * 4

        def gathers_until(part):
            return 16 * PER * PART_TILES * (part + 1)

        def stack_of(k):
            return x_stack[:, k % STACK_SLOTS, :].rearrange("p (r b) -> p r b", r=PER)

        def t_slot(stage):
            return t_ps[:, T_INDEX[stage] % T_SLOTS, :]

        def mlp_bank(tile):
            bank = mlp_ps[:] if tile < TILES - 1 else t_slot(("h1", tile, H1_ORDER[0]))[:, 0:BANK]
            return bank.rearrange("p (n b) -> p n b", b=P)

        def diag_units_until(step):
            return sum(u < FIRST_UNIT[step] for u in DIAG_UNITS)

        block = ctx.enter_context(nc.Block())

        @block.sync
        def _(sp):
            sp.dma_start(ids_sb[:], ids.rearrange("(t p) f -> p t f", p=P)).then_inc(ids_loaded, 16)
            def load_w(s):
                sp.dma_start(w_raw[s % RAW_SLOTS][:, 0:QUARTERS[s]],
                             w[P * PIECE_AT[s] // PER:P * PIECE_AT[s + 1] // PER].rearrange("(p c) -> p c", p=P)
                             ).then_inc(w_loaded[s % RAW_SLOTS], 16)

            for s in range(RAW_SLOTS):
                load_w(s)
            sp.dma_start(eye_sb[:], eye).then_inc(consts_loaded, 16)
            sp.dma_start(strips_sb[:], strips).then_inc(consts_loaded, 16)
            for s in range(PIECES):
                for ready, part, block in ((w_hi_ready, w_hi, 0), (w_lo_ready, w_lo, 2)):
                    sp.wait_ge(ready, s + 1)
                    if part is w_lo and s + RAW_SLOTS < PIECES:
                        load_w(s + RAW_SLOTS)
                    for q in range(PER):
                        at = PIECE_AT[s] + QUARTERS[s] * q
                        for b in (block, block + 1):
                            sp.dma_start(w_stack[EMB * b:EMB * (b + 1), at:at + QUARTERS[s]].bitcast(F32),
                                         part[EMB * q:EMB * (q + 1), s % 2, 0:QUARTERS[s]].bitcast(F32)
                                         ).then_inc(w_stacked[s], 16)
            sp.dma_start(z_diag[:, :, 0:DENSE], dense.rearrange("(t p) d -> p t d", p=P)
                         ).then_inc(dense_loaded, 16)
            for s in range(PIECES - 2, PIECES):
                sp.wait_ge(w_stacked[s], W_COPIES)
            full = (ROW_TILES * P + DIAG_K) // P
            rest = (ROW_TILES * P + DIAG_K) % P
            sp.dma_start(w1_sb[:, 0:full, :], w1[0:full * P].rearrange("(t p) n -> p t n", p=P)
                         ).then_inc(mlp_loaded, 16)
            sp.dma_start(w1_sb[0:rest, full, :], w1[full * P:]).then_inc(mlp_loaded, 16)
            sp.dma_start(w2_sb[:], w2.rearrange("(t p) n -> p t n", p=P)).then_inc(mlp_loaded, 16)
            sp.dma_start(w3_sb[:], w3).then_inc(mlp_loaded, 16)
            sp.dma_start(b1_sb[:], b1).then_inc(mlp_loaded, 16)
            sp.dma_start(b2_sb[:], b2).then_inc(mlp_loaded, 16)
            for tile in range(TILES):
                sp.wait_ge(y_ready, tile + 1)
                sp.dma_start(out[P * tile:P * (tile + 1)].rearrange("b o -> o b"), y_sb[:, tile % 2, :]
                             ).then_inc(stored[tile % 2], 16)
            for s in range(2):
                sp.wait_ge(stored[s], 16 * TILES // 2)

        @block.gpsimd
        def _(pool):
            pool.wait_ge(ids_loaded, 16)
            for part in range(PARTS):
                for f in range(FIELDS):
                    g = f // PER
                    if part > 0 and f % PER == 0:
                        pool.wait_ge(gathered[g], gathers_until(part - 1))
                    for t in range(PART_TILES * part, PART_TILES * (part + 1)):
                        pool.indirect_dma_start(
                            x[:, t, EMB * f:EMB * f + EMB], None, tables[f],
                            bass.IndirectOffsetOnAxis(ids_sb[:, t, f:f + 1].bitcast(U32), 0)
                        ).then_inc(gathered[g], 16)

        @block.scalar
        def _(act):
            act.wait_ge(consts_loaded, 32)
            act.copy(eye_r[:], eye_sb[:]).then_inc(consts_ready, 1)

            def w_is_stacked():
                for s in range(PIECES - 2, PIECES):
                    act.wait_ge(w_stacked[s], W_COPIES)

            for stage in PLAN:
                kind, k = stage[0], stage[1]
                if kind == "w_split":
                    act.wait_ge(w_loaded[k % RAW_SLOTS], 16 * (k // RAW_SLOTS + 1))
                    if k >= 2:
                        act.wait_ge(w_stacked[k - 2], W_COPIES)
                    act.copy(w_hi[:, k % 2, 0:QUARTERS[k]], w_raw[k % RAW_SLOTS][:, 0:QUARTERS[k]]
                             ).then_inc(w_hi_ready, 1)
                elif kind == "split":
                    part, g = divmod(k, GROUPS)
                    act.wait_ge(gathered[g], gathers_until(part))
                    if k >= PART_SLOTS:
                        act.wait_ge(side_filled, SIDE["stack", k - PART_SLOTS] + 1)
                    for t in range(PART_TILES):
                        group = x[:, PART_TILES * part + t, P * g:P * g + P].rearrange("p (r e) -> p r e", r=PER)
                        last = act.copy(x_parts[:, k % PART_SLOTS, t, :, 0:4:2, :],
                                        group.unsqueeze(2).to_broadcast([P, PER, 2, EMB]))
                    last.then_inc(x_hi_ready, 1)
                    act.wait_ge(x_lo_ready, k + 1)
                    act.copy(x_parts[:, k % PART_SLOTS, :, :, 3, :], x_parts[:, k % PART_SLOTS, :, :, 1, :]
                             ).then_inc(x_parts_ready, 1)
                elif kind == "stack":
                    act.wait_ge(side_filled, SIDE[stage] + 1)
                    if k >= STACK_SLOTS:
                        act.wait_ge(t_filled, FIRST_UNIT[k - STACK_SLOTS + 1])
                    act.copy(x_stack[:, k % STACK_SLOTS, :], t_slot(stage)).then_inc(side_drained, 1)
                elif kind == "turn":
                    part, g = divmod(k, GROUPS)
                    act.wait_ge(side_filled, SIDE[stage] + 1)
                    if k == GROUPS - 1 - LATE_TURNED:
                        w_is_stacked()
                    act.copy(x_turned[g][:, ROWS_B * part:ROWS_B * (part + 1)], t_slot(stage)[:, 0:ROWS_B]
                             ).then_inc(side_drained, 1)
                elif kind == "z_turn":
                    act.wait_ge(side_filled, SIDE[stage] + 1)
                    act.copy(z_t[-1][0:DIAG_K, ROWS_B * k:ROWS_B * (k + 1)], t_slot(stage)[0:DIAG_K, 0:ROWS_B]
                             ).then_inc(side_drained, 1)
                elif kind == "z_out":
                    part, tile = stage[1:]
                    act.wait_ge(rows_summed, (part * CHUNKS + min(32 * (tile + 1), CHUNKS)) // PER)
                    if part == 0 and tile == EARLY_Z:
                        w_is_stacked()
                    act.copy(z_t[tile][:, ROWS_B * part:ROWS_B * (part + 1)], z_ps[:, 0:ROWS_B]
                             ).then_inc(z_drained, 1)
                elif kind == "relu1":
                    act.wait_ge(mlp_loaded, 16 * 6)
                    act.wait_ge(h1_filled, k + 1)
                    for n in range(HID1 // P):
                        last = act.activation(h1[:, k % 2, n, :], mlp_bank(k)[:, n, :], ACT.Relu,
                                              bias=b1_sb[:, n:n + 1])
                    last.then_inc(h1_ready, 1)
                elif kind == "relu2":
                    act.wait_ge(h2_filled, k + 1)
                    for n in range(HID2 // P):
                        last = act.activation(h2[:, k % 2, n, :], mlp_bank(k)[:, n, :], ACT.Relu,
                                              bias=b2_sb[:, n:n + 1])
                    last.then_inc(h2_ready, 1)
                elif kind == "y":
                    act.wait_ge(y_filled, k + 1)
                    if k >= 2:
                        act.wait_ge(stored[k % 2], 16 * (k // 2))
                    act.copy(y_sb[:, k % 2, :], mlp_bank(k)[0:1, 0, :]).then_inc(y_ready, 1)

        @block.tensor
        def _(pe):
            pe.wait_ge(consts_ready, 1)
            for stage in PLAN:
                kind, k = stage[0], stage[1]
                if stage in T_INDEX and T_INDEX[stage] >= T_SLOTS:
                    before = T_JOBS[T_INDEX[stage] - T_SLOTS]
                    if before[0] == "unit":
                        pe.wait_ge(multiplied, before[1] + 1)
                    else:
                        pe.wait_ge(side_drained, SIDE[before] + 1)
                if kind == "stack":
                    pe.wait_ge(x_parts_ready, k + 1)
                    for c in range(PER * PART_TILES):
                        r, t = divmod(c, PART_TILES)
                        mm = pe.matmul(t_slot(stage)[:, P * c:P * c + P],
                                       x_parts[:, k % PART_SLOTS, t, r, :, :].rearrange("p s e -> p (s e)"), eye_r[:],
                                       start=True, stop=True)
                    mm.then_inc(side_filled, 1)
                elif kind == "turn":
                    part, g = divmod(k, GROUPS)
                    pe.wait_ge(gathered[g], gathers_until(part))
                    for t in range(PART_TILES):
                        mm = pe.matmul(t_slot(stage)[:, P * t:P * t + P],
                                       x[:, PART_TILES * part + t, P * g:P * g + P],
                                       eye_sb[:], is_transpose=True, start=True, stop=True)
                    mm.then_inc(side_filled, 1)
                elif kind == "unit":
                    what, step, a = UNITS[k]
                    part, g = divmod(step, GROUPS)
                    stack, dst = stack_of(step), t_slot(stage)
                    if k == FIRST_UNIT[step]:
                        pe.wait_ge(side_drained, SIDE["stack", step] + 1)
                        if part == 0:
                            for s in range(pieces_until(g - 1) if g > 0 else 0, pieces_until(g)):
                                pe.wait_ge(w_stacked[s], W_COPIES)
                    if what == "rows":
                        for r in range(PER):
                            at = w_at(g, a) + P * r
                            mm = pe.matmul(dst[:, ROWS_B * r:ROWS_B * (r + 1)], w_stack[:, at:at + P],
                                           stack[:, r, :], start=True, stop=True)
                    else:
                        for t in range(PART_TILES):
                            for r, c, n in ((1, 0, 1), (2, 1, 2), (3, 3, 3)):
                                at, to = w_at(g) + EMB * c, BANK // 2 * t + EMB * c
                                mm = pe.matmul(dst[:, to:to + EMB * n], stack[:, r, P * t:P * t + P],
                                               w_stack[:, at:at + EMB * n], start=True, stop=True)
                    mm.then_inc(t_filled, 1)
                elif kind == "sum":
                    _, step, a = UNITS[k]
                    pe.wait_ge(multiplied, k + 1)
                    for c in range(PER):
                        m = chunk_of(step, a) + c
                        strip, slot = m % 4, m % 32 // 4
                        before = step // GROUPS * ROW_TILES + m // 32
                        if m % 32 == 0 and before > 0:
                            pe.wait_ge(z_drained, before)
                        mm = pe.matmul(z_ps[EMB * strip:EMB * strip + EMB, 0:ROWS_B],
                                       strips_sb[:, EMB - PER - PER * slot:2 * EMB - PER - PER * slot],
                                       prod[:, k % PROD_SLOTS, ROWS_B * c:ROWS_B * (c + 1)],
                                       start=(slot == 0), stop=(slot == 7 or m >= CHUNKS - 4),
                                       skip_group_check=True, tile_position=(0, EMB * strip))
                    mm.then_inc(rows_summed, 1)
                elif kind == "z_turn":
                    pe.wait_ge(diag_summed, diag_units_until(GROUPS * (k + 1)))
                    pe.wait_ge(dense_loaded, 16)
                    for t in range(PART_TILES):
                        mm = pe.matmul(t_slot(stage)[0:DIAG_K, P * t:P * t + P], z_diag[:, PART_TILES * k + t, :],
                                       eye_sb[:], is_transpose=True, start=True, stop=True)
                    mm.then_inc(side_filled, 1)
                elif kind == "h1":
                    t, part = stage[2], k // PART_TILES
                    height = P if t < ROW_TILES else DIAG_K
                    if t == H1_ORDER[0]:
                        pe.wait_ge(mlp_loaded, 16 * 6)
                        if 0 < k < TILES - 1:
                            pe.wait_ge(y_ready, k)
                    if t < ROW_TILES:
                        pe.wait_ge(z_drained, ROW_TILES * part + t + 1)
                    else:
                        pe.wait_ge(side_drained, SIDE["z_turn", part] + 1)
                    for n in range(HID1 // P):
                        mm = pe.matmul(mlp_bank(k)[:, n, :], w1_sb[0:height, t, P * n:P * n + P],
                                       z_t[t][0:height, P * k:P * k + P], start=(t == H1_ORDER[0] and n == 0),
                                       stop=(t == H1_ORDER[-1]), skip_group_check=True)
                    if t == H1_ORDER[-1]:
                        mm.then_inc(h1_filled, 1)
                elif kind == "h2":
                    pe.wait_ge(h1_ready, k + 1)
                    for n in range(HID2 // P):
                        for t in range(HID1 // P):
                            mm = pe.matmul(mlp_bank(k)[:, n, :], w2_sb[:, t, P * n:P * n + P],
                                           h1[:, k % 2, t, :], start=(t == 0), stop=(t == HID1 // P - 1))
                    mm.then_inc(h2_filled, 1)
                elif kind == "y":
                    pe.wait_ge(h2_ready, k + 1)
                    for t in range(HID2 // P):
                        mm = pe.matmul(mlp_bank(k)[0:1, 0, :], w3_sb[:, t:t + 1], h2[:, k % 2, t, :],
                                       start=(t == 0), stop=(t == HID2 // P - 1))
                    mm.then_inc(y_filled, 1)

        @block.vector
        def _(dve):
            def sum_unit(u):
                part, g = divmod(UNITS[u][1], GROUPS)
                src = prod[:, u % PROD_SLOTS, 0:BANK // 2 * PART_TILES].rearrange(
                    "p (t c) -> p t c", t=PART_TILES)[:, :, 0:EMB * len(DIAG)].rearrange(
                    "p t (k e) -> p t k e", e=EMB)
                dve.wait_ge(multiplied, u + 1)
                dve.tensor_reduce(z_diag[:, PART_TILES * part:PART_TILES * (part + 1), z_at(g):z_at(g + 1)], src,
                                  AX_X, ALU.add).then_inc(diag_summed, 1)

            for stage in PLAN:
                kind, k = stage[0], stage[1]
                if kind == "w_split":
                    dve.wait_ge(w_hi_ready, k + 1)
                    if k >= 2:
                        dve.wait_ge(w_stacked[k - 2], W_COPIES)
                    dve.tensor_tensor(w_lo[:, k % 2, 0:QUARTERS[k]], w_raw[k % RAW_SLOTS][:, 0:QUARTERS[k]],
                                      w_hi[:, k % 2, 0:QUARTERS[k]], ALU.subtract).then_inc(w_lo_ready, 1)
                elif kind == "split":
                    part, g = divmod(k, GROUPS)
                    dve.wait_ge(gathered[g], gathers_until(part))
                    dve.wait_ge(x_hi_ready, k + 1)
                    group = x[:, PART_TILES * part:PART_TILES * (part + 1), P * g:P * g + P].rearrange(
                        "p t (r e) -> p t r e", r=PER)
                    dve.tensor_tensor(x_parts[:, k % PART_SLOTS, :, :, 1, :], group, x_parts[:, k % PART_SLOTS, :, :, 0, :],
                                      ALU.subtract).then_inc(x_lo_ready, 1)
                elif kind == "unit":
                    what, step, a = UNITS[k]
                    part, g = divmod(step, GROUPS)
                    tiles = slice(PART_TILES * part, PART_TILES * (part + 1))
                    if k >= PROD_SLOTS:
                        before = k - PROD_SLOTS
                        if UNITS[before][0] == "rows":
                            dve.wait_ge(rows_summed, SUM_INDEX["sum", before] + 1)
                        else:
                            dve.wait_ge(diag_summed, DIAG_INDEX[before] + 1)
                    if what == "rows":
                        dve.wait_ge(side_drained, SIDE["turn", GROUPS * part + a] + 1)
                    dve.wait_ge(t_filled, k + 1)
                    t_in, p_out = t_slot(stage), prod[:, k % PROD_SLOTS, :]
                    if what == "rows":
                        def view(y):
                            return y.rearrange("p (r b) -> p r b", r=PER)
                        other = x_turned[a][:, ROWS_B * part:ROWS_B * (part + 1)].unsqueeze(1).to_broadcast(
                            [P, PER, ROWS_B])
                        dve.tensor_tensor(view(p_out), view(t_in), other, ALU.mult).then_inc(multiplied, 1)
                    else:
                        def pairs(y):
                            return y[:, 0:BANK // 2 * PART_TILES].rearrange("p (t c) -> p t c", t=PART_TILES)[
                                :, :, 0:EMB * len(DIAG)]

                        def middle(y):
                            return pairs(y)[:, :, EMB:5 * EMB].rearrange("p t (s c) -> p t s c", s=2)

                        def ends(y):
                            return pairs(y).rearrange("p t (k e) -> p t k e", e=EMB)[:, :, 0:6:5, :]
                        mine = x[:, tiles, P * g:P * g + P]
                        both = mine[:, :, 0:2 * EMB].unsqueeze(2).to_broadcast([P, PART_TILES, 2, 2 * EMB])
                        even = mine.rearrange("p t (s c) -> p t s c", s=2)[:, :, :, 0:EMB]
                        dve.tensor_tensor(middle(p_out), middle(t_in), both, ALU.mult)
                        dve.tensor_tensor(ends(p_out), ends(t_in), even, ALU.mult).then_inc(multiplied, 1)
                    if k - 1 in DIAG_INDEX:
                        sum_unit(k - 1)
            assert len(UNITS) - 1 not in DIAG_INDEX


def kernel(**inputs):
    import concourse.bacc as bacc
    from concourse.bass_utils import run_bass_kernel_spmd

    a = {name: np.ascontiguousarray(value) for name, value in inputs.items()}
    index = {}
    for j in range(FIELDS):
        for i in range(j + 1, FIELDS):
            index[j, i] = len(index)
    blocks = []
    for g in range(GROUPS):
        blocks += [index[PER * o + s, PER * g + r] for o in range(g) for r in range(PER) for s in range(PER)]
        blocks += [index[PER * g + j, PER * g + i] for i, j in DIAG]
    w = a["L0_rec_W"][blocks].transpose(2, 0, 1).reshape(EMB, W_COLS)
    w = np.concatenate([w[:, PIECE_AT[n]:PIECE_AT[n + 1]].reshape(EMB, PER, QUARTERS[n]).transpose(1, 0, 2).ravel()
                        for n in range(PIECES)])
    z_rows, z_columns = pair_order()
    below = list(range(PAIRS, PAIRS + DENSE)) + [index[p] for p in z_columns]
    w1 = np.zeros((ROW_TILES * P + DIAG_K, HID1), np.float32)
    for row, pair in enumerate(z_rows):
        if pair is not None:
            w1[row] = a["W_top1"][index[pair]]
    w1[ROW_TILES * P:] = a["W_top1"][below]
    strips = np.zeros((P, 2 * EMB - PER), np.float32)
    for p in range(P):
        strips[p, EMB - PER + p // EMB] = 1.0
    laid = {
        "ids": a["ids"], **{f"tbl_{f}": a[f"tbl_{f}"] for f in range(FIELDS)},
        "dense": a["dense_ctx"], "w": w, "w1": w1,
        "b1": a["b_top1"].reshape(HID1 // P, P).T, "w2": a["W_top2"],
        "b2": a["b_top2"].reshape(HID2 // P, P).T, "w3": a["W_top3"].reshape(HID2 // P, P).T,
        "eye": np.eye(P, dtype=np.float32), "strips": strips,
    }
    nc = bacc.Bacc("TRN2", target_bir_lowering=False, num_devices=1)
    arrays, ap = {}, {}
    for name, value in laid.items():
        value = np.ascontiguousarray(value)
        arrays[f"{name}_dram"] = value
        ap[name] = nc.dram_tensor(f"{name}_dram", value.shape, mybir.dt.from_np(value.dtype),
                                  kind="ExternalInput").ap()
    out = nc.dram_tensor("y_dram", (BATCH, 1), F32, kind="ExternalOutput").ap()
    program(nc, ap["ids"], [ap[f"tbl_{f}"] for f in range(FIELDS)], ap["dense"], ap["w"],
            ap["w1"], ap["b1"], ap["w2"], ap["b2"], ap["w3"], ap["eye"], ap["strips"], out)
    got = run_bass_kernel_spmd(nc, [arrays], core_ids=[0])
    return got.results[0]["y_dram"]
```
